# Optimizing a Trainium2 kernel written in Bass

```python
import numpy as np
import jax
import jax.numpy as jnp

def _softmax(x, axis=-1):
    return jax.nn.softmax(x, axis=axis)

def _gelu(x):
    return jax.nn.gelu(x, approximate=True)

def _silu(x):
    return jax.nn.silu(x)

def _sigmoid(x):
    return jax.nn.sigmoid(x)

def _layernorm(x, axis=-1, eps=1e-05):
    m = jnp.mean(x, axis=axis, keepdims=True)
    v = jnp.var(x, axis=axis, keepdims=True)
    return (x - m) / jnp.sqrt(v + eps)

def _scatter_add(tgt, idx, src, axis=0):
    return tgt.at[idx].add(src)

def _segment_sum(src, seg, n):
    return jax.ops.segment_sum(src, seg, n)
kernel_name = 'mk_gps_d1_gnn_r8_5acfdd'

def setup_inputs(seed: int=0):
    np.random.seed(seed)
    _w = jnp.asarray

    def _rec_inputs():
        import jax
        import jax.numpy as jnp
        _gk = jax.random.key(seed)
        x = -0.0003713 + 1 * jax.random.normal(jax.random.fold_in(_gk, 1), (6250, 256), jnp.float32)
        src = jax.random.randint(jax.random.fold_in(_gk, 2), (200000,), 0, 6250, jnp.int32)
        dst = jax.random.randint(jax.random.fold_in(_gk, 3), (200000,), 0, 6250, jnp.int32)
        _o = jnp.argsort(dst, stable=True)
        src = src[_o]
        dst = dst[_o]
        return (x, src, dst)
    x, src, dst = _rec_inputs()

    def _L0_gnn_setup():
        import jax, jax.numpy as jnp
        import numpy as np
        HEAD = 8
        D = 128
        GIN = 256
        GOUT = 256
        N = 6250
        E = 100000

        def gt_layer(edge_index, embeds, qT, kT, vT, ln_s, ln_b):
            rows, cols = (edge_index[0], edge_index[1])
            n, d = embeds.shape
            hd = d // HEAD
            rowE = embeds[rows]
            colE = embeds[cols]
            q = (rowE @ qT).reshape(-1, HEAD, hd)
            k = (colE @ kT).reshape(-1, HEAD, hd)
            v = (colE @ vT).reshape(-1, HEAD, hd)
            att = jnp.clip(jnp.einsum('ehd,ehd->eh', q, k), -10.0, 10.0)
            expAtt = jnp.exp(att)
            attNorm = jax.ops.segment_sum(expAtt, rows, num_segments=n)[rows]
            att = expAtt / (attNorm + 1e-08)
            res = (att[..., None] * v).reshape(-1, d)
            agg = jax.ops.segment_sum(res, rows, num_segments=n)
            out = agg + embeds
            mu = jnp.mean(out, axis=-1, keepdims=True)
            var = jnp.mean((out - mu) ** 2, axis=-1, keepdims=True)
            return (out - mu) / jnp.sqrt(var + 1e-06) * ln_s + ln_b
        key = jax.random.key(seed)
        ks = jax.random.split(key, 16)

        def xavier(k, shape):
            lim = np.sqrt(6.0 / (shape[0] + shape[1]))
            return jax.random.uniform(k, shape, jnp.float32, -lim, lim)
        inp = {'x': jax.random.normal(ks[0], (N, GIN), jnp.float32), 'edge_index': jax.random.randint(ks[1], (2, E), 0, N, jnp.int64), 'W_P_w': xavier(ks[2], (GIN, D)), 'W_P_b': jnp.zeros((D,), jnp.float32), 'W_pos': jax.random.uniform(ks[3], (1, D), jnp.float32, -0.02, 0.02), 'q1': xavier(ks[4], (D, D)), 'k1': xavier(ks[5], (D, D)), 'v1': xavier(ks[6], (D, D)), 'ln1_s': jnp.ones((D,), jnp.float32), 'ln1_b': jnp.zeros((D,), jnp.float32), 'q2': xavier(ks[7], (D, D)), 'k2': xavier(ks[8], (D, D)), 'v2': xavier(ks[9], (D, D)), 'ln2_s': jnp.ones((D,), jnp.float32), 'ln2_b': jnp.zeros((D,), jnp.float32), 'inv_w': xavier(ks[10], (D, GOUT)), 'inv_b': jnp.zeros((GOUT,), jnp.float32)}
        return inp
    _L0_gnn_all = _L0_gnn_setup()
    _L0_gnn_in = {k: v for k, v in _L0_gnn_all.items() if k in ('W_P_w', 'W_P_b', 'W_pos', 'q1', 'k1', 'v1', 'ln1_s', 'ln1_b', 'q2', 'k2', 'v2', 'ln2_s', 'ln2_b', 'inv_w', 'inv_b')}
    del _L0_gnn_all

    def _L0_mix_setup():
        import jax, jax.numpy as jnp
        import numpy as np
        EPS_NORM = 1e-06
        EPS_ATTN = 1e-06
        HEADS = 8

        def rmsnorm(x, w):
            ms = jnp.mean(x * x, axis=-1, keepdims=True)
            return w * (x * jax.lax.rsqrt(ms + EPS_NORM))

        def linear_attention(x, w_qkv, w_out, b_out):
            B, N, D = x.shape
            hd = D // HEADS
            qkv = (x @ w_qkv).reshape(B, N, 3, HEADS, hd)
            q, k, v = (qkv[:, :, 0], qkv[:, :, 1], qkv[:, :, 2])
            q = jax.nn.elu(q) + 1.0
            k = jax.nn.elu(k) + 1.0
            kv = jnp.einsum('bnhd,bnhm->bhdm', k, v)
            z = 1.0 / (jnp.einsum('bnhd,bhd->bnh', q, k.sum(axis=1)) + EPS_ATTN)
            out = jnp.einsum('bnhd,bhdm,bnh->bnhm', q, kv, z)
            out = out.reshape(B, N, D)
            return out @ w_out + b_out
        key = jax.random.key(seed)
        ks = jax.random.split(key, 4)
        B, N, D = (16, 1024, 256)
        x = jax.random.normal(ks[0], (B, N, D), dtype=jnp.float32)
        w_norm1 = jnp.ones((D,), dtype=jnp.float32)
        w_qkv = jax.random.normal(ks[1], (D, 3 * D), dtype=jnp.float32) * 0.02
        w_out = jax.random.normal(ks[2], (D, D), dtype=jnp.float32) * 0.02
        b_out = jnp.zeros((D,), dtype=jnp.float32)
        w_norm2 = jnp.ones((D,), dtype=jnp.float32)
        return {'x': x, 'w_norm1': w_norm1, 'w_qkv': w_qkv, 'w_out': w_out, 'b_out': b_out, 'w_norm2': w_norm2}
    _L0_mix_all = _L0_mix_setup()
    _L0_mix_in = {k: v for k, v in _L0_mix_all.items() if k in ('w_norm1', 'w_qkv', 'w_out', 'b_out', 'w_norm2')}
    del _L0_mix_all

    def _L0_ffn_setup():
        import jax, jax.numpy as jnp
        import numpy as np
        B, N, D = (16, 512, 256)
        NUM_EXPERTS, TOP_K, HEADS = (4, 2, 4)
        N_EDGES = 131072
        LN_EPS = 1e-05

        def _layernorm(x, g, b):
            mu = x.mean(-1, keepdims=True)
            var = ((x - mu) ** 2).mean(-1, keepdims=True)
            return (x - mu) * jax.lax.rsqrt(var + LN_EPS) * g + b

        def _forward(x, edge_index, W_gat, att_src, att_dst, b_gat, ln_gamma, ln_beta, W1, b1, W2, b2):
            Bc, Nc, Dc = x.shape
            M = Bc * Nc
            x_flat = x.reshape(M, Dc)
            h = (x_flat @ W_gat).reshape(M, HEADS, NUM_EXPERTS)
            loops = jnp.arange(M, dtype=edge_index.dtype)
            src = jnp.concatenate([edge_index[0], loops])
            dst = jnp.concatenate([edge_index[1], loops])
            a_src = (h * att_src).sum(-1)
            a_dst = (h * att_dst).sum(-1)
            e = jax.nn.leaky_relu(a_src[src] + a_dst[dst], negative_slope=0.2)
            e_max = jax.ops.segment_max(e, dst, num_segments=M)
            ee = jnp.exp(e - e_max[dst])
            denom = jax.ops.segment_sum(ee, dst, num_segments=M)
            alpha = ee / (denom[dst] + 1e-16)
            msg = h[src] * alpha[:, :, None]
            agg = jax.ops.segment_sum(msg, dst, num_segments=M).reshape(M, HEADS * NUM_EXPERTS) + b_gat
            scores = _layernorm(agg, ln_gamma, ln_beta).reshape(M, HEADS, NUM_EXPERTS).mean(1)
            scores = scores.reshape(Bc, Nc, NUM_EXPERTS)
            topk_s, topk_i = jax.lax.top_k(scores, TOP_K)
            w = jax.nn.softmax(topk_s, axis=-1)
            out = jnp.zeros_like(x)
            for ei in range(NUM_EXPERTS):
                g = jnp.where(topk_i == ei, w, 0.0).sum(-1)
                hh = jax.nn.gelu(x @ W1[ei] + b1[ei], approximate=False)
                out = out + g[..., None] * (hh @ W2[ei] + b2[ei])
            return out
        key = jax.random.key(seed)
        ks = jax.random.split(key, 8)
        s = 0.05
        return {'x': jax.random.normal(ks[0], (B, N, D), jnp.float32), 'W_gat': jax.random.normal(ks[1], (D, HEADS * NUM_EXPERTS), jnp.float32) * s, 'att_src': jax.random.normal(ks[2], (HEADS, NUM_EXPERTS), jnp.float32) * s, 'att_dst': jax.random.normal(ks[3], (HEADS, NUM_EXPERTS), jnp.float32) * s, 'b_gat': jnp.zeros((HEADS * NUM_EXPERTS,), jnp.float32), 'ln_gamma': jnp.ones((HEADS * NUM_EXPERTS,), jnp.float32), 'ln_beta': jnp.zeros((HEADS * NUM_EXPERTS,), jnp.float32), 'W1': jax.random.normal(ks[4], (NUM_EXPERTS, D, 2 * D), jnp.float32) * s, 'b1': jnp.zeros((NUM_EXPERTS, 2 * D), jnp.float32), 'W2': jax.random.normal(ks[5], (NUM_EXPERTS, 2 * D, D), jnp.float32) * s, 'b2': jnp.zeros((NUM_EXPERTS, D), jnp.float32), 'edge_index': jax.random.randint(ks[6], (2, N_EDGES), 0, B * N, jnp.int32)}
    _L0_ffn_all = _L0_ffn_setup()
    _L0_ffn_in = {k: v for k, v in _L0_ffn_all.items() if k in ('W_gat', 'att_src', 'att_dst', 'b_gat', 'ln_gamma', 'ln_beta', 'W1', 'b1', 'W2', 'b2', 'edge_index')}
    del _L0_ffn_all
    return {'x': x, 'src': src, 'dst': dst, 'L0_gnn_W_P_w': _L0_gnn_in['W_P_w'], 'L0_gnn_W_P_b': _L0_gnn_in['W_P_b'], 'L0_gnn_W_pos': _L0_gnn_in['W_pos'], 'L0_gnn_q1': _L0_gnn_in['q1'], 'L0_gnn_k1': _L0_gnn_in['k1'], 'L0_gnn_v1': _L0_gnn_in['v1'], 'L0_gnn_ln1_s': _L0_gnn_in['ln1_s'], 'L0_gnn_ln1_b': _L0_gnn_in['ln1_b'], 'L0_gnn_q2': _L0_gnn_in['q2'], 'L0_gnn_k2': _L0_gnn_in['k2'], 'L0_gnn_v2': _L0_gnn_in['v2'], 'L0_gnn_ln2_s': _L0_gnn_in['ln2_s'], 'L0_gnn_ln2_b': _L0_gnn_in['ln2_b'], 'L0_gnn_inv_w': _L0_gnn_in['inv_w'], 'L0_gnn_inv_b': _L0_gnn_in['inv_b'], 'L0_mix_w_norm1': _L0_mix_in['w_norm1'], 'L0_mix_w_qkv': _L0_mix_in['w_qkv'], 'L0_mix_w_out': _L0_mix_in['w_out'], 'L0_mix_b_out': _L0_mix_in['b_out'], 'L0_mix_w_norm2': _L0_mix_in['w_norm2'], 'L0_ffn_W_gat': _L0_ffn_in['W_gat'], 'L0_ffn_att_src': _L0_ffn_in['att_src'], 'L0_ffn_att_dst': _L0_ffn_in['att_dst'], 'L0_ffn_b_gat': _L0_ffn_in['b_gat'], 'L0_ffn_ln_gamma': _L0_ffn_in['ln_gamma'], 'L0_ffn_ln_beta': _L0_ffn_in['ln_beta'], 'L0_ffn_W1': _L0_ffn_in['W1'], 'L0_ffn_b1': _L0_ffn_in['b1'], 'L0_ffn_W2': _L0_ffn_in['W2'], 'L0_ffn_b2': _L0_ffn_in['b2'], 'L0_ffn_edge_index': _L0_ffn_in['edge_index']}

def reference(x, src, dst, L0_gnn_W_P_w, L0_gnn_W_P_b, L0_gnn_W_pos, L0_gnn_q1, L0_gnn_k1, L0_gnn_v1, L0_gnn_ln1_s, L0_gnn_ln1_b, L0_gnn_q2, L0_gnn_k2, L0_gnn_v2, L0_gnn_ln2_s, L0_gnn_ln2_b, L0_gnn_inv_w, L0_gnn_inv_b, L0_mix_w_norm1, L0_mix_w_qkv, L0_mix_w_out, L0_mix_b_out, L0_mix_w_norm2, L0_ffn_W_gat, L0_ffn_att_src, L0_ffn_att_dst, L0_ffn_b_gat, L0_ffn_ln_gamma, L0_ffn_ln_beta, L0_ffn_W1, L0_ffn_b1, L0_ffn_W2, L0_ffn_b2, L0_ffn_edge_index):
    import jax
    import jax.numpy as jnp

    def _L0_gnn_ref(x, edge_index, W_P_w, W_P_b, W_pos, q1, k1, v1, ln1_s, ln1_b, q2, k2, v2, ln2_s, ln2_b, inv_w, inv_b):
        import jax, jax.numpy as jnp
        import numpy as np
        HEAD = 8
        D = 128
        GIN = 256
        GOUT = 256
        N = 6250
        E = 100000

        def gt_layer(edge_index, embeds, qT, kT, vT, ln_s, ln_b):
            rows, cols = (edge_index[0], edge_index[1])
            n, d = embeds.shape
            hd = d // HEAD
            rowE = embeds[rows]
            colE = embeds[cols]
            q = (rowE @ qT).reshape(-1, HEAD, hd)
            k = (colE @ kT).reshape(-1, HEAD, hd)
            v = (colE @ vT).reshape(-1, HEAD, hd)
            att = jnp.clip(jnp.einsum('ehd,ehd->eh', q, k), -10.0, 10.0)
            expAtt = jnp.exp(att)
            attNorm = jax.ops.segment_sum(expAtt, rows, num_segments=n)[rows]
            att = expAtt / (attNorm + 1e-08)
            res = (att[..., None] * v).reshape(-1, d)
            agg = jax.ops.segment_sum(res, rows, num_segments=n)
            out = agg + embeds
            mu = jnp.mean(out, axis=-1, keepdims=True)
            var = jnp.mean((out - mu) ** 2, axis=-1, keepdims=True)
            return (out - mu) / jnp.sqrt(var + 1e-06) * ln_s + ln_b
        z = x @ W_P_w + W_P_b
        embeds = z + W_pos
        embeds = gt_layer(edge_index, embeds, q1, k1, v1, ln1_s, ln1_b)
        embeds = gt_layer(edge_index, embeds, q2, k2, v2, ln2_s, ln2_b)
        return embeds @ inv_w + inv_b

    def _L0_mix_ref(x, w_norm1, w_qkv, w_out, b_out, w_norm2):
        import jax, jax.numpy as jnp
        import numpy as np
        EPS_NORM = 1e-06
        EPS_ATTN = 1e-06
        HEADS = 8

        def rmsnorm(x, w):
            ms = jnp.mean(x * x, axis=-1, keepdims=True)
            return w * (x * jax.lax.rsqrt(ms + EPS_NORM))

        def linear_attention(x, w_qkv, w_out, b_out):
            B, N, D = x.shape
            hd = D // HEADS
            qkv = (x @ w_qkv).reshape(B, N, 3, HEADS, hd)
            q, k, v = (qkv[:, :, 0], qkv[:, :, 1], qkv[:, :, 2])
            q = jax.nn.elu(q) + 1.0
            k = jax.nn.elu(k) + 1.0
            kv = jnp.einsum('bnhd,bnhm->bhdm', k, v)
            z = 1.0 / (jnp.einsum('bnhd,bhd->bnh', q, k.sum(axis=1)) + EPS_ATTN)
            out = jnp.einsum('bnhd,bhdm,bnh->bnhm', q, kv, z)
            out = out.reshape(B, N, D)
            return out @ w_out + b_out
        h = x + linear_attention(rmsnorm(x, w_norm1), w_qkv, w_out, b_out)
        return h + rmsnorm(h, w_norm2)

    def _L0_ffn_ref(x, W_gat, att_src, att_dst, b_gat, ln_gamma, ln_beta, W1, b1, W2, b2, edge_index):
        import jax, jax.numpy as jnp
        import numpy as np
        B, N, D = (16, 512, 256)
        NUM_EXPERTS, TOP_K, HEADS = (4, 2, 4)
        N_EDGES = 131072
        LN_EPS = 1e-05

        def _layernorm(x, g, b):
            mu = x.mean(-1, keepdims=True)
            var = ((x - mu) ** 2).mean(-1, keepdims=True)
            return (x - mu) * jax.lax.rsqrt(var + LN_EPS) * g + b

        def _forward(x, edge_index, W_gat, att_src, att_dst, b_gat, ln_gamma, ln_beta, W1, b1, W2, b2):
            Bc, Nc, Dc = x.shape
            M = Bc * Nc
            x_flat = x.reshape(M, Dc)
            h = (x_flat @ W_gat).reshape(M, HEADS, NUM_EXPERTS)
            loops = jnp.arange(M, dtype=edge_index.dtype)
            src = jnp.concatenate([edge_index[0], loops])
            dst = jnp.concatenate([edge_index[1], loops])
            a_src = (h * att_src).sum(-1)
            a_dst = (h * att_dst).sum(-1)
            e = jax.nn.leaky_relu(a_src[src] + a_dst[dst], negative_slope=0.2)
            e_max = jax.ops.segment_max(e, dst, num_segments=M)
            ee = jnp.exp(e - e_max[dst])
            denom = jax.ops.segment_sum(ee, dst, num_segments=M)
            alpha = ee / (denom[dst] + 1e-16)
            msg = h[src] * alpha[:, :, None]
            agg = jax.ops.segment_sum(msg, dst, num_segments=M).reshape(M, HEADS * NUM_EXPERTS) + b_gat
            scores = _layernorm(agg, ln_gamma, ln_beta).reshape(M, HEADS, NUM_EXPERTS).mean(1)
            scores = scores.reshape(Bc, Nc, NUM_EXPERTS)
            topk_s, topk_i = jax.lax.top_k(scores, TOP_K)
            w = jax.nn.softmax(topk_s, axis=-1)
            out = jnp.zeros_like(x)
            for ei in range(NUM_EXPERTS):
                g = jnp.where(topk_i == ei, w, 0.0).sum(-1)
                hh = jax.nn.gelu(x @ W1[ei] + b1[ei], approximate=False)
                out = out + g[..., None] * (hh @ W2[ei] + b2[ei])
            return out
        return _forward(x, edge_index, W_gat, att_src, att_dst, b_gat, ln_gamma, ln_beta, W1, b1, W2, b2)
    edge_index = jnp.stack([src, dst])
    xn = _layernorm(x, axis=-1)
    x = x + _L0_gnn_ref(xn, edge_index, L0_gnn_W_P_w, L0_gnn_W_P_b, L0_gnn_W_pos, L0_gnn_q1, L0_gnn_k1, L0_gnn_v1, L0_gnn_ln1_s, L0_gnn_ln1_b, L0_gnn_q2, L0_gnn_k2, L0_gnn_v2, L0_gnn_ln2_s, L0_gnn_ln2_b, L0_gnn_inv_w, L0_gnn_inv_b) + _L0_mix_ref(xn[None], L0_mix_w_norm1, L0_mix_w_qkv, L0_mix_w_out, L0_mix_b_out, L0_mix_w_norm2)[0]
    x = x + _L0_ffn_ref(_layernorm(x, axis=-1)[None], L0_ffn_W_gat, L0_ffn_att_src, L0_ffn_att_dst, L0_ffn_b_gat, L0_ffn_ln_gamma, L0_ffn_ln_beta, L0_ffn_W1, L0_ffn_b1, L0_ffn_W2, L0_ffn_b2, L0_ffn_edge_index)[0]
    return x

_drawn_inputs = setup_inputs


def setup_inputs(seed=0):
    import zlib

    import numpy as np

    out = dict(_drawn_inputs(seed))
    spreads = {'L0_gnn_W_P_b': (0.0, 0.1),
     'L0_gnn_ln1_s': (1.0, 0.2),
     'L0_gnn_ln1_b': (0.0, 0.1),
     'L0_gnn_ln2_s': (1.0, 0.2),
     'L0_gnn_ln2_b': (0.0, 0.1),
     'L0_gnn_inv_b': (0.0, 0.1),
     'L0_mix_w_norm1': (1.0, 0.6),
     'L0_mix_b_out': (0.0, 0.1),
     'L0_mix_w_norm2': (1.0, 0.2),
     'L0_ffn_b_gat': (0.0, 0.1),
     'L0_ffn_ln_gamma': (1.0, 0.2),
     'L0_ffn_ln_beta': (0.0, 0.1),
     'L0_ffn_b1': (0.0, 0.477),
     'L0_ffn_b2': (0.0, 0.36)}
    factors = {'L0_gnn_W_pos': 5.111, 'L0_mix_w_qkv': 8.0, 'L0_mix_w_out': 8.0, 'L0_ffn_att_dst': 4.373}
    for name, (base, spread) in spreads.items():
        noise = np.random.default_rng([zlib.crc32(name.encode()), seed]).standard_normal(out[name].shape)
        drawn = base * np.exp(spread * noise) if base else spread * noise
        out[name] = jnp.asarray(drawn.astype(out[name].dtype))
    for name, factor in factors.items():
        out[name] = (out[name] * factor).astype(out[name].dtype)
    return out
```

```python
from contextlib import ExitStack, contextmanager

import numpy as np

import concourse.bass as bass
from concourse import mybir

ALU = mybir.AluOpType
ACT = mybir.ActivationFunctionType
AX = mybir.AxisListType.X
F32 = mybir.dt.float32
BF16 = mybir.dt.bfloat16
I32 = mybir.dt.int32

LANES = 128
PAIR = 2
NODE_TILE = 125
COLS = 16
GROUP = 4
SLOTS = 4


class Constants:
    pass


class Chain:

    def __init__(self, eng, sem):
        self.eng, self.sem, self.n = eng, sem, 0

    def __call__(self, ins):
        ins.then_inc(self.sem, 1)
        self.n = self.n + 1
        self.eng.wait_ge(self.sem, self.n)

    @contextmanager
    def loop(self, count, per):
        base = self.n
        with self.eng.Fori(0, count, 1) as i:
            self.n = i * per + base
            yield i
        self.n = base + count * per


class Graph:

    def __init__(self, nc, name, key, other, edges, parts, nodes, keys):
        self.name, self.key, self.other = name, key, other
        self.parts, self.cols = parts, edges // parts
        assert parts * self.cols == edges and self.cols % COLS == 0
        self.tiles = nodes // NODE_TILE
        self.buckets = self.tiles + (keys > nodes)
        self.nodes, self.keys = nodes, keys
        bound = (edges + self.buckets * (PAIR * LANES - 1)) // (PAIR * LANES)
        self.pairs = -(-bound // 8) * 8
        self.edge_tiles = PAIR * self.pairs
        self.spread = next(p for p in range(LANES, 0, -1) if self.pairs % p == 0)
        self.table = nc.dram_tensor(f"{name}_table", [LANES * self.edge_tiles, 2], I32, kind="Internal").ap()
        self.pair_tile = nc.dram_tensor(f"{name}_pair_tile", [self.pairs], I32, kind="Internal").ap()


def place_tensors(nc, ctx, g, rec=None):
    def sb(name, shape, dt=F32):
        return ctx.enter_context(nc.sbuf_tensor(f"{g.name}_{name}", shape, dt))

    g.key_sb = sb("key_sb", [g.parts, g.cols], I32)
    g.other_sb = sb("other_sb", [g.parts, g.cols], I32)
    g.digit_i = sb("digit_i", [g.parts, g.cols], I32)
    g.digit = sb("digit", [g.parts, g.cols], BF16)
    g.mask = sb("mask", [g.parts, g.cols], BF16)
    g.junk = sb("junk", [g.parts, g.cols], BF16)
    g.scan = sb("scan", [g.parts, g.cols])
    g.pos = sb("pos", [g.parts, g.cols])
    g.below = sb("below", [g.parts, g.buckets + 1])
    g.count = sb("count", [g.parts, g.buckets])
    g.pairs_i = sb("pairs_i", [LANES, g.buckets], I32)
    g.pairs_f = sb("pairs_f", [LANES, g.buckets])
    g.pair_end = sb("pair_end", [LANES, g.buckets])
    g.start = sb("start", [g.parts, g.buckets])
    g.pt = sb("pt", [g.spread, g.pairs // g.spread])
    g.pt_i = sb("pt_i", [g.spread, g.pairs // g.spread], I32)
    g.pair_no = sb("pair_no", [g.spread, g.pairs // g.spread])


def place_vector(dve, chain, g, c, sems):
    n = g.buckets
    dve.wait_ge(sems["edges_in"], 32)
    chain(dve.tensor_scalar(g.digit_i[:], g.key_sb[:], 1.0 / NODE_TILE, 0.5 / NODE_TILE - 0.5, ALU.mult, ALU.add))
    dve.tensor_scalar(g.digit[:], g.digit_i[:], float(n - 1), None, ALU.min).then_inc(sems["digits"], 1)
    dve.wait_ge(sems["digits"], 1)
    chain(dve.scalar_tensor_tensor(out=g.scan[:], in0=g.digit[:], scalar=-float(NODE_TILE), in1=g.key_sb[:],
                                   op0=ALU.mult, op1=ALU.add))
    if n > g.tiles:
        chain(dve.tensor_scalar(g.pos[:], g.digit[:], float(g.tiles), float(g.keys), ALU.is_ge, ALU.mult))
        chain(dve.tensor_tensor(g.rec[:, :, 2], g.scan[:], g.pos[:], ALU.add))
    else:
        chain(dve.tensor_copy(g.rec[:, :, 2], g.scan[:]))
    chain(dve.tensor_scalar(g.rec[:, :, 1], g.other_sb[:], float(g.nodes - 1), None, ALU.min))
    chain(dve.memset(g.pos[:], 0.0))
    dve.wait_ge(sems["counted"], n + 1)
    chain(dve.tensor_tensor(g.count[:], g.below[:, 0:n], g.below[:, 1:n + 1], ALU.subtract))
    dve.tensor_scalar(g.count[:], g.count[:], 0.5, None, ALU.mult).then_inc(sems["counts"], 1)
    dve.wait_ge(sems["totals"], 1)
    chain(dve.tensor_scalar(g.pairs_i[:], g.ps_total[:, 0:n], float(PAIR * LANES - 1), None, ALU.add))
    chain(dve.tensor_scalar(g.pairs_i[:], g.pairs_i[:], 8, None, ALU.arith_shift_right))
    chain(dve.tensor_copy(g.pairs_f[:], g.pairs_i[:]))
    chain(dve.tensor_tensor_scan(g.pair_end[:], g.pairs_f[:], g.pairs_f[:], 0.0, ALU.add, ALU.max))
    p = g.parts
    chain(dve.tensor_tensor(g.start[:], g.pair_end[0:p], g.pairs_f[0:p], ALU.subtract))
    chain(dve.scalar_tensor_tensor(out=g.start[:], in0=g.start[:], scalar=float(PAIR * LANES),
                                   in1=g.ps_before[0:p, 0:n], op0=ALU.mult, op1=ALU.add))
    chain(dve.memset(g.pt[:], 0.0))
    dve.wait_ge(sems["empty"], 1)
    with chain.loop(n, 1) as b:
        chain(dve.scalar_tensor_tensor(out=g.pt[:], in0=g.pair_no[:], scalar=g.pair_end[0:g.spread, bass.ds(b, 1)],
                                       in1=g.pt[:], op0=ALU.is_ge, op1=ALU.add))
    dve.tensor_scalar(g.pt_i[:], g.pt[:], float(g.tiles - 1), None, ALU.min).then_inc(sems["pair_tiles"], 1)
    with chain.loop(n, 4) as b:
        chain(dve.tensor_scalar(g.mask[:], g.digit[:], c.number[0:p, bass.ds(b, 1)], None, ALU.is_equal))
        chain(dve.tensor_tensor_scan(g.scan[:], g.mask[:], g.mask[:], g.start[:, bass.ds(b, 1)], ALU.add, ALU.max))
        chain(dve.tensor_tensor(g.scan[:], g.scan[:], g.mask[:], ALU.mult))
        chain(dve.tensor_tensor(g.pos[:], g.pos[:], g.scan[:], ALU.add))
    chain(dve.tensor_scalar(g.digit_i[:], g.pos[:], 1.0, None, ALU.subtract))
    chain(dve.tensor_scalar(g.key_sb[:], g.digit_i[:], LANES - 1, None, ALU.bitwise_and))
    chain(dve.tensor_scalar(g.digit_i[:], g.digit_i[:], 7, None, ALU.arith_shift_right))
    dve.scalar_tensor_tensor(out=g.rec[:, :, 0], in0=g.key_sb[:], scalar=float(g.edge_tiles), in1=g.digit_i[:],
                             op0=ALU.mult, op1=ALU.add).then_inc(sems["placed"], 1)


def place_scalar(act, chain, g, c, sems):
    act.wait_ge(sems["digits"], 1)
    with chain.loop(g.buckets + 1, 1) as b:
        ins = act.activation(g.junk[:], g.digit[:], ACT.Sign, bias=c.half_less[0:g.parts, bass.ds(b, 1)],
                             accum_out=g.below[:, bass.ds(b, 1)])
        chain(ins)


def place_tensor(pe, g, c, sems):
    pe.wait_ge(sems["counts"], 1)
    p, n = g.parts, g.buckets
    pe.matmul(g.ps_before[0:p, 0:n], c.earlier[0:p, 0:p], g.count[:], start=True, stop=True)
    pe.matmul(g.ps_total[:, 0:n], c.ones[0:p, :], g.count[:], start=True, stop=True).then_inc(sems["totals"], 1)


def scatter_stage(sp, g, stage, sems):
    def fill(i, h):
        sp.dma_start(stage[0:g.parts, h], g.rec[:, bass.ds((i * 2 + h) * COLS, COLS), :])\
            .then_inc(sems["staged"][h], 16)

    sp.wait_ge(sems["placed"], 1)
    for h in range(2):
        fill(0, h)
    with sp.Fori(1, g.cols // COLS // 2, 1) as i:
        for h in range(2):
            sp.wait_ge(sems["moved"][h], i * (COLS * 16))
            sp.nop(nofuse=True)
            fill(i, h)


def scatter_pool(pool, g, stage, sems):
    pool.wait_ge(sems["cleared"], 16)
    rounds = g.cols // COLS // 2
    with pool.Fori(0, rounds, 1) as i:
        for h in range(2):
            pool.wait_ge(sems["staged"][h], (i + 1) * 16)
            pool.nop(nofuse=True)
            for k in range(COLS):
                pool.indirect_dma_start(
                    g.table, bass.IndirectOffsetOnAxis(ap=stage[0:g.parts, h, k, 0:1], axis=0),
                    stage[0:g.parts, h, k, 1:3], None).then_inc(sems["moved"][h], 16)
    for h in range(2):
        pool.wait_ge(sems["moved"][h], rounds * COLS * 16)


@contextmanager
def semaphores(nc, names):
    handles = [nc.alloc_semaphore(name=n) for n in names]
    yield handles
    nc.clear_and_free_semaphores(handles)
    nc.all_engine_barrier()


def sem_set(nc, ctx, prefix, names):
    handles = ctx.enter_context(semaphores(nc, [f"{prefix}_{n}" for n in names]))
    return dict(zip(names, handles))


PLACE_SEMS = ["edges_in", "digits", "counted", "counts", "totals", "pair_tiles", "pair_tiles_out", "placed",
              "empty", "cleared", "chain"]


def load_edges(q, g, sems):
    q.dma_start(g.key_sb[:], g.key.rearrange("(p n) -> p n", p=g.parts)).then_inc(sems["edges_in"], 16)
    q.dma_start(g.other_sb[:], g.other.rearrange("(p n) -> p n", p=g.parts)).then_inc(sems["edges_in"], 16)


def constants(nc, ctx):
    def sb(name, shape, dt=F32):
        return ctx.enter_context(nc.sbuf_tensor(name, shape, dt))

    c = Constants()
    c.number = sb("number", [LANES, 64])
    c.half_less = sb("half_less", [LANES, 64])
    c.earlier = sb("earlier", [LANES, LANES])
    c.ones = sb("ones", [LANES, LANES])
    c.ident = sb("ident", [LANES, LANES])
    c.node_no = sb("node_no", [LANES, GROUP, NODE_TILE])
    c.ident16 = sb("ident16", [LANES, LANES], BF16)
    c.same_head = sb("same_head", [LANES, LANES])
    c.eps5 = sb("eps5", [LANES, 1])
    c.eps6 = sb("eps6", [LANES, 1])
    c.pick_head = sb("pick_head", [SPLIT * FH, FH, NODE_TILE], BF16)
    with ExitStack() as st:
        ready, = st.enter_context(semaphores(nc, ["const_steps"]))
        block = st.enter_context(nc.Block())

        @block.gpsimd
        def _(pool):
            chain = Chain(pool, ready)
            chain(pool.iota(c.number[:], [[1, 64]], base=0, channel_multiplier=0, allow_small_or_imprecise_dtypes=True))
            chain(pool.tensor_scalar(c.half_less[:], c.number[:], -1.0, 0.5, ALU.mult, ALU.add))
            chain(pool.iota(c.node_no[:], [[0, GROUP], [1, NODE_TILE]], base=0, channel_multiplier=0,
                            allow_small_or_imprecise_dtypes=True))
            chain(pool.memset(c.ones[:], 1.0))
            chain(pool.memset(c.eps5[:], 1e-5))
            chain(pool.memset(c.eps6[:], 1e-6))
            chain(pool.memset(c.same_head[:], 0.0))
            for h in range(LANES // 32):
                chain(pool.memset(c.same_head[h * 32:(h + 1) * 32, h * 32:(h + 1) * 32], 1.0))
            chain(pool.memset(c.pick_head[:], 0.0))
            for n in range(SPLIT):
                chain(pool.affine_select(out=c.pick_head[:], in_=c.pick_head[:], compare_op=ALU.not_equal, fill=1.0,
                                         base=-n * FH, pattern=[[-1, FH], [0, NODE_TILE]], channel_multiplier=1))
            chain(pool.affine_select(out=c.ident[:], in_=c.ones[:], compare_op=ALU.is_equal, fill=0.0, base=0,
                                     pattern=[[-1, LANES]], channel_multiplier=1))
            chain(pool.tensor_copy(c.ident16[:], c.ident[:]))
            chain(pool.affine_select(out=c.earlier[:], in_=c.ones[:], compare_op=ALU.is_gt, fill=0.0, base=0,
                                     pattern=[[1, LANES]], channel_multiplier=-1))
    return c


def place_sp(sp, g, sems):
    sp.wait_ge(sems["empty"], 1)
    sp.dma_start(g.table.rearrange("(p n) e -> p n e", p=LANES), g.empty[:]).then_inc(sems["cleared"], 16)
    sp.wait_ge(sems["pair_tiles"], 1)
    sp.dma_start(g.pair_tile.rearrange("(p n) -> p n", p=g.spread), g.pt_i[:]).then_inc(sems["pair_tiles_out"], 16)
    sp.wait_ge(sems["pair_tiles_out"], 16)


def place_pool(pool, g, sems, chain):
    w = g.pairs // g.spread
    chain(pool.iota(g.pair_no[:], [[1, w]], base=0, channel_multiplier=w, allow_small_or_imprecise_dtypes=True))
    chain(pool.memset(g.empty[:], 0))
    pool.memset(g.empty[:, :, 1], -1).then_inc(sems["empty"], 1)


def place(nc, c, graphs):
    with ExitStack() as st:
        sets = []
        for g in graphs:
            g.rec = st.enter_context(nc.sbuf_tensor(f"{g.name}_rec", [g.parts, g.cols, 3], I32))
            g.stage = st.enter_context(nc.sbuf_tensor(f"{g.name}_stage", [LANES, 2, COLS, 3], I32))
            place_tensors(nc, st, g)
            g.empty = st.enter_context(nc.sbuf_tensor(f"{g.name}_empty", [LANES, g.edge_tiles, 2], I32))
            g.ps_before = st.enter_context(nc.psum_tensor(f"{g.name}_ps_before", [LANES, 512], F32))
            g.ps_total = st.enter_context(nc.psum_tensor(f"{g.name}_ps_total", [LANES, 512], F32))
            sems = sem_set(nc, st, g.name, PLACE_SEMS + ["pool_chain"])
            sems["staged"] = st.enter_context(semaphores(nc, [f"{g.name}_staged{h}" for h in range(2)]))
            sems["moved"] = c.moved[g.name]
            sets.append((g, sems))
        block = st.enter_context(nc.Block())

        @block.vector
        def _(dve):
            for g, sems in sets:
                place_vector(dve, Chain(dve, sems["chain"]), g, c, sems)

        @block.scalar
        def _(act):
            for g, sems in sets:
                load_edges(act, g, sems)
            for g, sems in sets:
                place_scalar(act, Chain(act, sems["counted"]), g, c, sems)

        @block.tensor
        def _(pe):
            for g, sems in sets:
                place_tensor(pe, g, c, sems)

        @block.sync
        def _(sp):
            for g, sems in sets:
                place_sp(sp, g, sems)
                scatter_stage(sp, g, g.stage, sems)

        @block.gpsimd
        def _(pool):
            for g, sems in sets:
                place_pool(pool, g, sems, Chain(pool, sems["pool_chain"]))
            for g, sems in sets:
                scatter_pool(pool, g, g.stage, sems)


def at(tensor, t):
    return tensor[:, t] if isinstance(t, int) else tensor[:, bass.ds(t, 1)].squeeze(1)


def at2(tensor, t):
    return tensor[:, t:t + 1] if isinstance(t, int) else tensor[:, bass.ds(t, 1)]


def at_row(rows, t):
    return rows[t] if isinstance(t, int) else rows[bass.ds(t, 1)].squeeze(0)


def wait(eng, sem, value):
    if not isinstance(value, int) or value > 0:
        eng.wait_ge(sem, value)


def pipeline(eng, total, slots, parts):
    lags = [lag for lag, _ in parts]

    def step(round_, offset):
        for lag, part in parts:
            n = offset + lag
            if isinstance(round_, int) and not 0 <= round_ * slots + n < total:
                continue
            part(round_ * slots + n, round_ + n // slots, n % slots)

    first = -(-4 // slots)
    rounds = (total - max(lags)) // slots
    for s in range(-max(lags), first * slots):
        step(0, s)
    with eng.Fori(first, rounds, 1) as i:
        for s in range(slots):
            step(i, s)
    for s in range(rounds * slots, total - min(lags)):
        step(0, s)


def edge_steps(eng, total, parts):
    pipeline(eng, total, SLOTS, parts)


def node_steps(eng, total, parts):
    pipeline(eng, total, 2, parts)


def stage_slots(sp, g, stage, sems, gathered=None):
    table = g.table.rearrange("(p n) e -> p n e", p=LANES)

    def part(k, r, j):
        if gathered is not None:
            wait(sp, gathered[j], r * (16 * GROUP))
            sp.nop(nofuse=True)
        wait(sp, sems["one_hots"], (k - SLOTS) + 1)
        sp.nop(nofuse=True)
        sp.dma_start(stage[:, j], table[:, bass.ds(k * GROUP, GROUP), :]).then_inc(sems["staged"][j], 16)
    edge_steps(sp, g.edge_tiles // GROUP, [(0, part)])


def gather_rows(pool, g, stage, rows, source, sems, used, also=None):
    def part(k, r, j):
        for read in (used, also):
            if read is not None:
                wait(pool, read, (k - SLOTS) + 1)
                pool.nop(nofuse=True)
        pool.wait_ge(sems["staged"][j], (r + 1) * 16)
        pool.nop(nofuse=True)
        for e in range(GROUP):
            pool.indirect_dma_start(rows(k, j, e), None, source,
                                    bass.IndirectOffsetOnAxis(ap=stage[:, j, e, 0:1], axis=0))\
                .then_inc(sems["gathered"][j], 16)
    edge_steps(pool, g.edge_tiles // GROUP, [(0, part)])


HEADS, HEAD = 8, 16
D = HEADS * HEAD
SUMS = D + HEADS


def project(nc, c, name, E, weights, qs, kv):
    tiles = E.shape[1]
    with ExitStack() as st:
        def sb(n, shape, dt=F32):
            return st.enter_context(nc.sbuf_tensor(f"{name}_{n}", shape, dt))

        def psum(n):
            return st.enter_context(nc.psum_tensor(f"{name}_{n}", [LANES, 512], F32))

        w = sb("w", [D, 3 * D])
        E_tile = sb("E_tile", [NODE_TILE, 2, D])
        ET = sb("ET", [D, 2, NODE_TILE])
        rest = sb("rest", [NODE_TILE, 2, D])
        kv_sb = sb("kv_sb", [NODE_TILE, 2, 2 * D])
        ps_t = [psum(f"ps_t{h}") for h in range(2)]
        ps_p = [psum(f"ps_p{h}") for h in range(2)]
        m = sem_set(nc, st, name, ["w_in", "taken", "turned", "turned_sb", "projected", "high", "split", "kv_copied",
                                   "middle", "low"])
        stored = st.enter_context(semaphores(nc, [f"{name}_stored{h}" for h in range(2)]))
        block = st.enter_context(nc.Block())

        @block.tensor
        def _(pe):
            pe.wait_ge(m["w_in"], 48)

            def turn(t, r, h):
                pe.wait_ge(m["taken"], t + 1)
                wait(pe, m["turned_sb"], t - 1)
                pe.transpose(ps_t[h][:, 0:NODE_TILE], E_tile[:, h, :], c.ident[0:NODE_TILE, 0:NODE_TILE])\
                    .then_inc(m["turned"], 1)

            def times_w(t, r, h):
                pe.wait_ge(m["turned_sb"], t + 1)
                wait(pe, m["kv_copied"], t - 1)
                pe.matmul(ps_p[h][0:NODE_TILE, 0:3 * D], ET[:, h, :], w[:], start=True, stop=True)\
                    .then_inc(m["projected"], 1)
            node_steps(pe, tiles, [(1, times_w), (2, turn)])

        @block.scalar
        def _(act):
            for n, weight in enumerate(weights):
                act.dma_start(w[:, n * D:(n + 1) * D], weight).then_inc(m["w_in"], 16)

            def take(t, r, h):
                wait(act, m["turned"], t - 1)
                act.nop(nofuse=True)
                act.copy(E_tile[:, h, :], at(E, t)).then_inc(m["taken"], 1)

            def copy_turned(t, r, h):
                act.wait_ge(m["turned"], t + 1)
                wait(act, m["projected"], t - 1)
                act.copy(ET[:, h, :], ps_t[h][:, 0:NODE_TILE]).then_inc(m["turned_sb"], 1)

            def copy_kv(t, r, h):
                act.wait_ge(m["split"], t + 1)
                wait(act, stored[h], r * 16)
                act.copy(kv_sb[:, h, :], ps_p[h][0:NODE_TILE, D:3 * D]).then_inc(m["kv_copied"], 1)
            node_steps(act, tiles, [(2, copy_turned), (3, take), (0, copy_kv)])

        @block.vector
        def _(dve):
            def high(t, r, h):
                dve.wait_ge(m["projected"], t + 1)
                dve.tensor_copy(at(qs, t)[:, 0, :], ps_p[h][0:NODE_TILE, 0:D]).then_inc(m["high"], 1)

            def split(t, r, h):
                dve.wait_ge(m["high"], t + 1)
                wait(dve, m["low"], t - 1)
                dve.tensor_tensor(rest[:, h, :], ps_p[h][0:NODE_TILE, 0:D], at(qs, t)[:, 0, :], ALU.subtract)\
                    .then_inc(m["split"], 1)

            def middle(t, r, h):
                dve.wait_ge(m["split"], t + 1)
                dve.tensor_copy(at(qs, t)[:, 1, :], rest[:, h, :]).then_inc(m["middle"], 1)

            def low(t, r, h):
                dve.wait_ge(m["middle"], t + 1)
                dve.tensor_tensor(at(qs, t)[:, 2, :], rest[:, h, :], at(qs, t)[:, 1, :], ALU.subtract)\
                    .then_inc(m["low"], 1)
            node_steps(dve, tiles, [(1, high), (0, middle), (1, split), (0, low)])

        @block.sync
        def _(sp):
            rows = kv.rearrange("(t p) d -> t p d", p=NODE_TILE)

            def store(t, r, h):
                sp.wait_ge(m["kv_copied"], t + 1)
                sp.nop(nofuse=True)
                sp.dma_start(at_row(rows, t), kv_sb[:, h, :]).then_inc(stored[h], 16)
            node_steps(sp, tiles, [(0, store)])
            for h in range(2):
                sp.wait_ge(stored[h], 16 * (tiles // 2))


def attend(nc, c, name, g, qs, kv, acc):
    with ExitStack() as st:
        def sb(n, shape, dt=F32):
            return st.enter_context(nc.sbuf_tensor(f"{name}_{n}", shape, dt))

        def psum(n):
            return [st.enter_context(nc.psum_tensor(f"{name}_{n}{h}", [LANES, 512], F32)) for h in range(2)]

        stage = sb("stage", [LANES, SLOTS, GROUP, 2], I32)
        kv_e = sb("kv_e", [LANES, SLOTS, GROUP, 2 * D])
        hot = sb("hot", [LANES, SLOTS, GROUP, NODE_TILE])
        hot_t = sb("hot_t", [NODE_TILE, 2, GROUP * LANES], BF16)
        prod = sb("prod", [LANES, 2, GROUP * D])
        dots_sb = sb("dots", [LANES, 2, GROUP * HEADS])
        clipped = sb("clipped", [LANES, 2, GROUP * HEADS])
        vals = sb("vals", [LANES, 2, GROUP, SUMS])
        tile_of = sb("tile_of", [1, g.pairs], I32)
        ps_hot, ps_q, ps_sum = psum("ps_hot"), psum("ps_q"), psum("ps_sum")
        m = sem_set(nc, st, name, ["tiles_in", "cleared", "one_hots", "turned", "turned_sb", "q_ready", "prods",
                                   "dots", "clips", "exps", "weighted", "summed", "added"])
        m["staged"] = st.enter_context(semaphores(nc, [f"{name}_staged{j}" for j in range(SLOTS)]))
        m["gathered"] = c.gathered[name]
        total = g.edge_tiles // GROUP
        block = st.enter_context(nc.Block())

        def node_tile(eng, pair):
            return eng.value_load(tile_of[0:1, bass.ds(pair, 1)], min_val=0, max_val=g.tiles - 1)

        @block.sync
        def _(sp):
            sp.dma_start(tile_of[:], g.pair_tile.rearrange("(a n) -> a n", a=1)).then_inc(m["tiles_in"], 16)
            stage_slots(sp, g, stage, m, m["gathered"])

        @block.gpsimd
        def _(pool):
            gather_rows(pool, g, stage, lambda k, j, e: kv_e[:, j, e, :], kv, m, used=m["weighted"])

        @block.tensor
        def _(pe):
            pe.wait_ge(m["tiles_in"], 16)

            def turn(k, r, j):
                pe.wait_ge(m["one_hots"], k + 1)
                wait(pe, m["turned_sb"], k - 1)
                for e in range(GROUP):
                    ins = pe.transpose(ps_hot[j % 2][0:NODE_TILE, e * LANES:(e + 1) * LANES], hot[:, j, e, :],
                                       c.ident[:])
                ins.then_inc(m["turned"], 1)

            def fetch_q(k, r, j):
                pe.wait_ge(m["turned_sb"], k + 1)
                wait(pe, m["prods"], k - 1)
                for p in range(GROUP // PAIR):
                    t = node_tile(pe, k * (GROUP // PAIR) + p)
                    for e in range(PAIR * p, PAIR * (p + 1)):
                        for part in range(3):
                            ins = pe.matmul(ps_q[j % 2][:, e * D:(e + 1) * D],
                                            hot_t[:, j % 2, e * LANES:(e + 1) * LANES],
                                            at(qs, t)[:, part, :], start=part == 0, stop=part == 2)
                ins.then_inc(m["q_ready"], 1)

            def add_up(k, r, j):
                pe.wait_ge(m["weighted"], k + 1)
                wait(pe, m["added"], 2 * (k - 2) + 2)
                for p in range(GROUP // PAIR):
                    for e in range(PAIR):
                        ins = pe.matmul(ps_sum[j % 2][0:NODE_TILE, p * 256:p * 256 + SUMS],
                                        hot[:, j, PAIR * p + e, :], vals[:, j % 2, PAIR * p + e, :],
                                        start=e == 0, stop=e == PAIR - 1)
                ins.then_inc(m["summed"], 1)
            edge_steps(pe, total, [(-2, add_up), (1, fetch_q), (2, turn)])

        @block.scalar
        def _(act):
            def copy_turned(k, r, j):
                act.wait_ge(m["turned"], k + 1)
                wait(act, m["q_ready"], k - 1)
                act.copy(hot_t[:, j % 2, :], ps_hot[j % 2][0:NODE_TILE, :]).then_inc(m["turned_sb"], 1)

            def exps(k, r, j):
                act.wait_ge(m["clips"], k + 1)
                wait(act, m["summed"], k - 1)
                act.activation(vals[:, j % 2, :, D:SUMS],
                               clipped[:, j % 2, :].rearrange("p (e h) -> p e h", e=GROUP), ACT.Exp)\
                    .then_inc(m["exps"], 1)
            edge_steps(act, total, [(2, copy_turned), (0, exps)])

        @block.vector
        def _(dve):
            dve.memset(acc[:], 0.0).then_inc(m["cleared"], 1)
            dve.wait_ge(m["tiles_in"], 16)
            dve.wait_ge(m["cleared"], 1)

            def dots(k, r, j):
                dve.wait_ge(m["q_ready"], k + 1)
                dve.wait_ge(m["gathered"][j], (r + 1) * (16 * GROUP))
                wait(dve, m["dots"], k - 1)
                dve.tensor_tensor(prod[:, j % 2, :].rearrange("p (e d) -> p e d", e=GROUP),
                                  ps_q[j % 2][:, :].rearrange("p (e d) -> p e d", e=GROUP),
                                  kv_e[:, j, :, 0:D], ALU.mult).then_inc(m["prods"], 1)

            def one_hot(k, r, j):
                dve.wait_ge(m["staged"][j], (r + 1) * 16)
                wait(dve, m["summed"], (k - SLOTS) + 1)
                dve.tensor_tensor(hot[:, j], c.node_no[:],
                                  stage[:, j, :, 1:2].broadcast_to([LANES, GROUP, NODE_TILE]), ALU.is_equal)\
                    .then_inc(m["one_hots"], 1)

            def sum_dots(k, r, j):
                dve.wait_ge(m["prods"], k + 1)
                wait(dve, m["clips"], k - 1)
                dve.tensor_reduce(dots_sb[:, j % 2, :], prod[:, j % 2, :].rearrange("p (h d) -> p h d", d=HEAD),
                                  AX, ALU.add).then_inc(m["dots"], 1)

            def weigh(k, r, j):
                dve.wait_ge(m["exps"], k + 1)
                dve.tensor_tensor(vals[:, j % 2, :, 0:D].rearrange("p e (h d) -> p e h d", d=HEAD),
                                  kv_e[:, j, :, D:2 * D].rearrange("p e (h d) -> p e h d", d=HEAD),
                                  vals[:, j % 2, :, D:SUMS].unsqueeze(3).broadcast_to([LANES, GROUP, HEADS, HEAD]),
                                  ALU.mult).then_inc(m["weighted"], 1)

            def clip(k, r, j):
                dve.wait_ge(m["dots"], k + 1)
                wait(dve, m["exps"], k - 1)
                dve.tensor_scalar(clipped[:, j % 2, :], dots_sb[:, j % 2, :], -10.0, 10.0, ALU.max, ALU.min)\
                    .then_inc(m["clips"], 1)

            def add_sums(k, r, j):
                dve.wait_ge(m["summed"], k + 1)
                for p in range(GROUP // PAIR):
                    t = node_tile(dve, k * (GROUP // PAIR) + p)
                    a = at(acc, t)
                    wait(dve, m["added"], 2 * k + p)
                    dve.tensor_tensor(a, a, ps_sum[j % 2][0:NODE_TILE, p * 256:p * 256 + SUMS], ALU.add)\
                        .then_inc(m["added"], 1)
            edge_steps(dve, total, [(0, dots), (2, one_hot), (0, sum_dots), (-1, weigh), (0, clip), (-2, add_sums)])


GIN = 256
KC = GIN // LANES
TILE_ROWS = "(t p) d -> p t d"


def over(row, tiles):
    return row.unsqueeze(1).broadcast_to([row.shape[0], tiles, row.shape[1]])


def each(value, width):
    return value.unsqueeze(2).broadcast_to([value.shape[0], value.shape[1], width])


def load_row(q, tensor, row, sem):
    q.dma_start(tensor, row.partition_broadcast(tensor.shape[0])).then_inc(sem, 16)


def row_statistics(nc, c, name, X, width, mean, rstd, var, eps, source=None):
    tiles = X.shape[1]
    per = 5
    with ExitStack() as st:
        def sb(n, shape):
            return st.enter_context(nc.sbuf_tensor(f"{name}_{n}", shape, F32))

        stats = sb("stats", [NODE_TILE, tiles, 6])
        gap = sb("gap", [NODE_TILE, tiles])
        m = sem_set(nc, st, name, ["loaded", "chain", "var_ready", "std_ready"])
        block = st.enter_context(nc.Block())

        @block.sync
        def _(sp):
            if source is not None:
                sp.dma_start(X[:], source).then_inc(m["loaded"], 16)

        @block.vector
        def _(dve):
            chain = Chain(dve, m["chain"])
            if source is not None:
                dve.wait_ge(m["loaded"], 16)
            with chain.loop(tiles // per, 1) as i:
                for t in range(per):
                    ins = dve.bn_stats(at(stats, i * per + t), at(X, i * per + t))
                chain(ins)
            chain(dve.tensor_tensor(mean[:], stats[:, :, 1], stats[:, :, 4], ALU.add))
            chain(dve.tensor_scalar(mean[:], mean[:], 0.5, None, ALU.mult))
            chain(dve.tensor_tensor(gap[:], stats[:, :, 1], stats[:, :, 4], ALU.subtract))
            chain(dve.tensor_tensor(gap[:], gap[:], gap[:], ALU.mult))
            chain(dve.tensor_tensor(var[:], stats[:, :, 2], stats[:, :, 5], ALU.add))
            chain(dve.tensor_scalar(var[:], var[:], 1.0 / width, None, ALU.mult))
            dve.scalar_tensor_tensor(out=var[:], in0=gap[:], scalar=0.25, in1=var[:], op0=ALU.mult, op1=ALU.add)\
                .then_inc(m["var_ready"], 1)
            dve.wait_ge(m["std_ready"], 1)
            chain(dve.reciprocal(rstd[:], rstd[:]))

        @block.scalar
        def _(act):
            act.wait_ge(m["var_ready"], 1)
            act.activation(rstd[:], var[:], ACT.Sqrt, bias=eps[0:NODE_TILE, 0:1]).then_inc(m["std_ready"], 1)


def embed(nc, c, ins, X, mean, rstd, mix_rstd, E, key_values, key_sums):
    tiles = X.shape[1]
    with ExitStack() as st:
        def sb(n, shape, dt=F32):
            return st.enter_context(nc.sbuf_tensor(f"embed_{n}", shape, dt))

        def psum(n):
            return [st.enter_context(nc.psum_tensor(f"embed_{n}{h}", [LANES, 512], F32)) for h in range(2)]

        wp = sb("wp", [LANES, KC, D])
        wkv = sb("wkv", [LANES, KC, 2 * GIN])
        w1 = sb("w1", [LANES, KC])
        bias = sb("bias", [NODE_TILE, D])
        pos = sb("pos", [NODE_TILE, D])
        xn = sb("xn", [NODE_TILE, 2, 2, GIN])
        xT = sb("xT", [LANES, 2, 2, KC, NODE_TILE])
        k_raw = sb("k_raw", [NODE_TILE, 2, GIN])
        k_exp = sb("k_exp", [NODE_TILE, 2, GIN])
        k = sb("k", [NODE_TILE, 2, GIN])
        v = sb("v", [NODE_TILE, 2, KC, LANES + 1])
        ps_t, ps_e, ps_kv, ps_sum = psum("ps_t"), psum("ps_e"), psum("ps_kv"), psum("ps_sum")
        m = sem_set(nc, st, "embed", ["w_in", "w_ready", "ones", "normed", "turned", "turned_sb", "projected", "e_out",
                                      "k_copied", "v_copied", "k_min", "k_exped", "k_ready", "summed", "chain"])
        block = st.enter_context(nc.Block())

        @block.sync
        def _(sp):
            sp.dma_start(wp[:], ins["L0_gnn_W_P_w"].rearrange("(c p) n -> p c n", p=LANES)).then_inc(m["w_in"], 16)
            sp.dma_start(wkv[:], ins["L0_mix_w_qkv"][:, GIN:3 * GIN].rearrange("(c p) n -> p c n", p=LANES))\
                .then_inc(m["w_in"], 16)
            sp.dma_start(w1[:], ins["L0_mix_w_norm1"].rearrange("(c p) -> p c", p=LANES),
                         allow_slow_non_contiguous=True).then_inc(m["w_in"], 16)
            load_row(sp, bias[:], ins["L0_gnn_W_P_b"], m["w_in"])
            load_row(sp, pos[:], ins["L0_gnn_W_pos"].rearrange("a n -> (a n)"), m["w_in"])

        @block.vector
        def _(dve):
            chain = Chain(dve, m["chain"])
            dve.wait_ge(m["w_in"], 80)
            chain(dve.tensor_tensor(bias[:], bias[:], pos[:], ALU.add))
            for ch in range(KC):
                chain(dve.tensor_scalar(wkv[:, ch, :], wkv[:, ch, :], w1[:, ch:ch + 1], None, ALU.mult))
            dve.memset(v[:, :, :, LANES:LANES + 1], 1.0).then_inc(m["w_ready"], 1)

            def norm(t, r, h):
                wait(dve, m["turned"], t - 1)
                dve.tensor_scalar(xn[:, h, 0, :], at(X, t), at2(mean, t), at2(rstd, t), ALU.subtract, ALU.mult)
                dve.tensor_scalar(xn[:, h, 1, :], at(X, t), at2(mean, t), at2(mix_rstd, t), ALU.subtract, ALU.mult)\
                    .then_inc(m["normed"], 1)

            def e_out(t, r, h):
                dve.wait_ge(m["projected"], t + 1)
                dve.tensor_tensor(at(E, t), ps_e[h][0:NODE_TILE, 0:D], bias[:], ALU.add).then_inc(m["e_out"], 1)

            def k_min(t, r, h):
                dve.wait_ge(m["k_copied"], t + 1)
                wait(dve, m["k_exped"], t - 1)
                wait(dve, m["k_ready"], t - 1)
                dve.tensor_scalar(k_exp[:, h, :], k_raw[:, h, :], 0.0, None, ALU.min).then_inc(m["k_min"], 1)

            def k_out(t, r, h):
                dve.wait_ge(m["k_exped"], t + 1)
                wait(dve, m["summed"], t - 1)
                dve.scalar_tensor_tensor(out=k[:, h, :], in0=k_raw[:, h, :], scalar=0.0, in1=k_exp[:, h, :],
                                         op0=ALU.max, op1=ALU.add).then_inc(m["k_ready"], 1)
            node_steps(dve, tiles, [(2, norm), (0, e_out), (-1, k_out), (0, k_min)])
            dve.wait_ge(m["summed"], tiles)
            for ch in range(KC):
                chain(dve.tensor_tensor(key_values[:, ch, :], ps_sum[ch][:, 0:LANES], c.same_head[:], ALU.mult))
                chain(dve.tensor_scalar(key_sums[:, ch, :], c.same_head[:], ps_sum[ch][:, LANES:LANES + 1], None,
                                        ALU.mult))

        @block.tensor
        def _(pe):
            pe.wait_ge(m["w_ready"], 1)

            def turn(t, r, h):
                pe.wait_ge(m["normed"], t + 1)
                wait(pe, m["turned_sb"], t - 1)
                for n in range(2 * KC):
                    ins = pe.transpose(ps_t[h][:, n * NODE_TILE:(n + 1) * NODE_TILE],
                                       xn[:, h, n // KC, n % KC * LANES:(n % KC + 1) * LANES],
                                       c.ident[0:NODE_TILE, 0:NODE_TILE])
                ins.then_inc(m["turned"], 1)

            def times_w(t, r, h):
                pe.wait_ge(m["turned_sb"], t + 1)
                wait(pe, m["e_out"], t - 1)
                wait(pe, m["v_copied"], t - 1)
                for ch in range(KC):
                    pe.matmul(ps_e[h][0:NODE_TILE, 0:D], xT[:, h, 0, ch, :], wp[:, ch, :], start=ch == 0,
                              stop=ch == KC - 1)
                for ch in range(KC):
                    ins = pe.matmul(ps_kv[h][0:NODE_TILE, :], xT[:, h, 1, ch, :], wkv[:, ch, :], start=ch == 0,
                                    stop=ch == KC - 1)
                ins.then_inc(m["projected"], 1)

            def sum_up(t, r, h):
                pe.wait_ge(m["k_ready"], t + 1)
                for ch in range(KC):
                    ins = pe.matmul(ps_sum[ch][:, 0:LANES + 1], k[:, h, ch * LANES:(ch + 1) * LANES], v[:, h, ch, :],
                                    start=isinstance(t, int) and t == 0, stop=isinstance(t, int) and t == tiles - 1)
                ins.then_inc(m["summed"], 1)
            node_steps(pe, tiles, [(-2, sum_up), (0, times_w), (1, turn)])

        @block.scalar
        def _(act):
            def copy_turned(t, r, h):
                act.wait_ge(m["turned"], t + 1)
                wait(act, m["projected"], t - 1)
                act.copy(xT[:, h], ps_t[h][:, 0:2 * KC * NODE_TILE].rearrange("p (a c n) -> p a c n", a=2, c=KC))\
                    .then_inc(m["turned_sb"], 1)

            def copy_kv(t, r, h):
                act.wait_ge(m["projected"], t + 1)
                wait(act, m["k_ready"], t - 1)
                act.copy(k_raw[:, h, :], ps_kv[h][0:NODE_TILE, 0:GIN]).then_inc(m["k_copied"], 1)
                wait(act, m["summed"], t - 1)
                act.copy(v[:, h, :, 0:LANES], ps_kv[h][0:NODE_TILE, GIN:2 * GIN].rearrange("p (c n) -> p c n", c=KC))\
                    .then_inc(m["v_copied"], 1)

            def k_exp_of(t, r, h):
                act.wait_ge(m["k_min"], t + 1)
                act.activation(k_exp[:, h, :], k_exp[:, h, :], ACT.Exp).then_inc(m["k_exped"], 1)
            node_steps(act, tiles, [(0, copy_kv), (1, copy_turned), (0, k_exp_of)])


def mix(nc, c, ins, X, mean, rstd, mean_rstd, mix_rstd, key_values, key_sums, H):
    tiles = X.shape[1]
    two = KC * NODE_TILE
    with ExitStack() as st:
        def sb(n, shape, dt=F32):
            return st.enter_context(nc.sbuf_tensor(f"mix_{n}", shape, dt))

        def psum(n):
            return [st.enter_context(nc.psum_tensor(f"mix_{n}{h}", [LANES, 512], F32)) for h in range(2)]

        wq = sb("wq", [LANES, KC, GIN])
        wo = sb("wo", [LANES, KC, GIN])
        w1 = sb("w1", [LANES, KC])
        xr = sb("xr", [NODE_TILE, 2, GIN])
        xT = sb("xT", [LANES, 2, KC, NODE_TILE])
        q_raw = sb("q_raw", [LANES, 2, two])
        q_exp = sb("q_exp", [LANES, 2, two])
        q = sb("q", [LANES, 2, two])
        den = sb("den", [LANES, 2, two])
        o = sb("o", [LANES, 2, two])
        ps_t, ps_q, ps_o, ps_h = psum("ps_t"), psum("ps_q"), psum("ps_o"), psum("ps_h")
        m = sem_set(nc, st, "mix", ["w_in", "w_ready", "normed", "turned", "turned_sb", "q_ps", "q_copied", "q_min",
                                    "q_exped", "q_ready", "o_ps", "den", "inverse", "o_ready", "h_ps", "h_base",
                                    "h_out", "chain"])
        block = st.enter_context(nc.Block())

        @block.sync
        def _(sp):
            sp.dma_start(wq[:], ins["L0_mix_w_qkv"][:, 0:GIN].rearrange("(c p) n -> p c n", p=LANES))\
                .then_inc(m["w_in"], 16)
            sp.dma_start(wo[:], ins["L0_mix_w_out"].rearrange("(c p) n -> p c n", p=LANES)).then_inc(m["w_in"], 16)
            sp.dma_start(w1[:], ins["L0_mix_w_norm1"].rearrange("(c p) -> p c", p=LANES),
                         allow_slow_non_contiguous=True).then_inc(m["w_in"], 16)

        @block.vector
        def _(dve):
            dve.wait_ge(m["w_in"], 48)
            for ch in range(KC):
                dve.tensor_scalar(wq[:, ch, :], wq[:, ch, :], w1[:, ch:ch + 1], None, ALU.mult).then_inc(m["w_ready"], 1)

            def norm(t, r, h):
                wait(dve, m["turned"], t - 1)
                dve.tensor_scalar(xr[:, h, :], at(X, t), at2(mean, t), at2(mix_rstd, t), ALU.subtract, ALU.mult)\
                    .then_inc(m["normed"], 1)

            def q_min(t, r, h):
                dve.wait_ge(m["q_copied"], t + 1)
                wait(dve, m["q_ready"], t - 1)
                dve.tensor_scalar(q_exp[:, h, :], q_raw[:, h, :], 0.0, None, ALU.min).then_inc(m["q_min"], 1)

            def q_out(t, r, h):
                dve.wait_ge(m["q_exped"], t + 1)
                wait(dve, m["o_ps"], t - 1)
                dve.scalar_tensor_tensor(out=q[:, h, :], in0=q_raw[:, h, :], scalar=0.0, in1=q_exp[:, h, :],
                                         op0=ALU.max, op1=ALU.add).then_inc(m["q_ready"], 1)

            def den_of(t, r, h):
                dve.wait_ge(m["o_ps"], t + 1)
                dve.tensor_scalar(den[:, h, :], ps_o[h][:, two:2 * two], 1e-6, None, ALU.add).then_inc(m["den"], 1)

            def inverse(t, r, h):
                dve.wait_ge(m["den"], t + 1)
                dve.reciprocal(den[:, h, :], den[:, h, :]).then_inc(m["inverse"], 1)

            def o_out(t, r, h):
                dve.wait_ge(m["inverse"], t + 1)
                wait(dve, m["h_ps"], t - 1)
                dve.tensor_tensor(o[:, h, :], ps_o[h][:, 0:two], den[:, h, :], ALU.mult).then_inc(m["o_ready"], 1)

            def h_out(t, r, h):
                dve.wait_ge(m["h_ps"], t + 1)
                dve.wait_ge(m["h_base"], t + 1)
                dve.tensor_tensor(at(H, t), at(H, t), ps_h[h][0:NODE_TILE, 0:GIN], ALU.add).then_inc(m["h_out"], 1)
            node_steps(dve, tiles, [(-1, den_of), (2, norm), (-1, inverse), (0, q_min), (-1, o_out), (-2, h_out),
                                    (0, q_out)])

        @block.tensor
        def _(pe):
            pe.wait_ge(m["w_ready"], 2)

            def turn(t, r, h):
                pe.wait_ge(m["normed"], t + 1)
                wait(pe, m["turned_sb"], t - 1)
                for ch in range(KC):
                    ins = pe.transpose(ps_t[h][:, ch * NODE_TILE:(ch + 1) * NODE_TILE],
                                       xr[:, h, ch * LANES:(ch + 1) * LANES], c.ident[0:NODE_TILE, 0:NODE_TILE])
                ins.then_inc(m["turned"], 1)

            def q_of(t, r, h):
                pe.wait_ge(m["turned_sb"], t + 1)
                wait(pe, m["q_copied"], t - 1)
                for d in range(KC):
                    for ch in range(KC):
                        ins = pe.matmul(ps_q[h][:, d * NODE_TILE:(d + 1) * NODE_TILE],
                                        wq[:, ch, d * LANES:(d + 1) * LANES], xT[:, h, ch, :], start=ch == 0,
                                        stop=ch == KC - 1)
                ins.then_inc(m["q_ps"], 1)

            def out_of(t, r, h):
                pe.wait_ge(m["q_ready"], t + 1)
                wait(pe, m["o_ready"], t - 1)
                for n, table in enumerate((key_values, key_sums)):
                    for ch in range(KC):
                        a = n * two + ch * NODE_TILE
                        ins = pe.matmul(ps_o[h][:, a:a + NODE_TILE], table[:, ch, :],
                                        q[:, h, ch * NODE_TILE:(ch + 1) * NODE_TILE], start=True, stop=True)
                ins.then_inc(m["o_ps"], 1)

            def h_of(t, r, h):
                pe.wait_ge(m["o_ready"], t + 1)
                wait(pe, m["h_out"], t - 1)
                for ch in range(KC):
                    ins = pe.matmul(ps_h[h][0:NODE_TILE, 0:GIN], o[:, h, ch * NODE_TILE:(ch + 1) * NODE_TILE],
                                    wo[:, ch, :], start=ch == 0, stop=ch == KC - 1)
                ins.then_inc(m["h_ps"], 1)
            node_steps(pe, tiles, [(-1, out_of), (-2, h_of), (1, q_of), (2, turn)])

        @block.scalar
        def _(act):
            def copy_turned(t, r, h):
                act.wait_ge(m["turned"], t + 1)
                wait(act, m["q_ps"], t - 1)
                act.copy(xT[:, h], ps_t[h][:, 0:two].rearrange("p (c n) -> p c n", c=KC)).then_inc(m["turned_sb"], 1)

            def copy_q(t, r, h):
                act.wait_ge(m["q_ps"], t + 1)
                wait(act, m["q_ready"], t - 1)
                act.copy(q_raw[:, h, :], ps_q[h][:, 0:two]).then_inc(m["q_copied"], 1)

            def q_exp_of(t, r, h):
                act.wait_ge(m["q_min"], t + 1)
                act.activation(q_exp[:, h, :], q_exp[:, h, :], ACT.Exp).then_inc(m["q_exped"], 1)

            def base(t, r, h):
                act.activation(at(H, t), at(X, t), ACT.Identity, scale=at2(rstd, t), bias=at2(mean_rstd, t))\
                    .then_inc(m["h_base"], 1)
            node_steps(act, tiles, [(0, base), (0, q_exp_of), (1, copy_q), (2, copy_turned)])


def mix_finish(nc, c, ins, X, H, tmp):
    tiles = X.shape[1]
    with ExitStack() as st:
        b = st.enter_context(nc.sbuf_tensor("fin_b", [NODE_TILE, GIN], F32))
        w2 = st.enter_context(nc.sbuf_tensor("fin_w2", [NODE_TILE, GIN], F32))
        ms = st.enter_context(nc.sbuf_tensor("fin_ms", [NODE_TILE, tiles], F32))
        m = sem_set(nc, st, "fin", ["w_in", "chain", "ms_ready", "root_ready"])
        block = st.enter_context(nc.Block())

        @block.sync
        def _(sp):
            load_row(sp, b[:], ins["L0_mix_b_out"], m["w_in"])
            load_row(sp, w2[:], ins["L0_mix_w_norm2"], m["w_in"])

        @block.vector
        def _(dve):
            chain = Chain(dve, m["chain"])
            dve.wait_ge(m["w_in"], 32)
            chain(dve.tensor_tensor(H[:], H[:], over(b[:], tiles), ALU.add))
            chain(dve.tensor_tensor(tmp[:], H[:], H[:], ALU.mult))
            chain(dve.tensor_tensor(X[:], X[:], H[:], ALU.add))
            dve.tensor_reduce(ms[:], tmp[:], AX, ALU.add).then_inc(m["ms_ready"], 1)
            dve.wait_ge(m["ms_ready"], 1)
            chain(dve.tensor_tensor(tmp[:], H[:], over(w2[:], tiles), ALU.mult))
            dve.wait_ge(m["root_ready"], 1)
            chain(dve.reciprocal(ms[:], ms[:]))
            chain(dve.tensor_tensor(tmp[:], tmp[:], each(ms[:], GIN), ALU.mult))
            chain(dve.tensor_tensor(X[:], X[:], tmp[:], ALU.add))

        @block.scalar
        def _(act):
            act.wait_ge(m["ms_ready"], 1)
            act.activation(ms[:], ms[:], ACT.Sqrt, scale=1.0 / GIN, bias=c.eps6[0:NODE_TILE, :]).then_inc(m["root_ready"], 1)


def mix_scales(nc, c, mean, rstd, var, mean_rstd, mix_rstd):
    with ExitStack() as st:
        m = sem_set(nc, st, "scales", ["chain", "ms_ready", "root_ready"])
        block = st.enter_context(nc.Block())

        @block.vector
        def _(dve):
            chain = Chain(dve, m["chain"])
            chain(dve.scalar_tensor_tensor(out=mean_rstd[:], in0=mean[:], scalar=-1.0, in1=rstd[:], op0=ALU.mult,
                                           op1=ALU.mult))
            chain(dve.tensor_tensor(mix_rstd[:], rstd[:], rstd[:], ALU.mult))
            dve.tensor_tensor(mix_rstd[:], mix_rstd[:], var[:], ALU.mult).then_inc(m["ms_ready"], 1)
            dve.wait_ge(m["root_ready"], 1)
            chain(dve.reciprocal(mix_rstd[:], mix_rstd[:]))
            chain(dve.tensor_tensor(mix_rstd[:], mix_rstd[:], rstd[:], ALU.mult))

        @block.scalar
        def _(act):
            act.wait_ge(m["ms_ready"], 1)
            act.activation(mix_rstd[:], mix_rstd[:], ACT.Sqrt, bias=c.eps6[0:NODE_TILE, :]).then_inc(m["root_ready"], 1)


def attended(nc, c, name, acc, E, tmp, scale, shift):
    tiles = E.shape[1]
    with ExitStack() as st:
        s = st.enter_context(nc.sbuf_tensor(f"{name}_s", [NODE_TILE, D], F32))
        b = st.enter_context(nc.sbuf_tensor(f"{name}_b", [NODE_TILE, D], F32))
        mean = st.enter_context(nc.sbuf_tensor(f"{name}_mean", [NODE_TILE, tiles], F32))
        var = st.enter_context(nc.sbuf_tensor(f"{name}_var", [NODE_TILE, tiles], F32))
        m = sem_set(nc, st, name, ["w_in", "chain", "var_ready", "root_ready"])
        block = st.enter_context(nc.Block())

        @block.sync
        def _(sp):
            load_row(sp, s[:], scale, m["w_in"])
            load_row(sp, b[:], shift, m["w_in"])

        @block.vector
        def _(dve):
            chain = Chain(dve, m["chain"])
            weights = acc[:, :, D:SUMS]
            chain(dve.tensor_scalar(weights, weights, 1e-8, None, ALU.add))
            chain(dve.reciprocal(weights, weights))
            for h in range(HEADS):
                part = acc[:, :, h * HEAD:(h + 1) * HEAD]
                last = dve.tensor_tensor(part, part, acc[:, :, D + h:D + h + 1].broadcast_to([NODE_TILE, tiles, HEAD]),
                                         ALU.mult)
            chain(last)
            chain(dve.tensor_tensor(E[:], E[:], acc[:, :, 0:D], ALU.add))
            chain(dve.tensor_reduce(mean[:], E[:], AX, ALU.add))
            chain(dve.tensor_scalar(mean[:], mean[:], 1.0 / D, None, ALU.mult))
            chain(dve.tensor_tensor(E[:], E[:], each(mean[:], D), ALU.subtract))
            chain(dve.tensor_tensor(tmp[:], E[:], E[:], ALU.mult))
            dve.tensor_reduce(var[:], tmp[:], AX, ALU.add).then_inc(m["var_ready"], 1)
            dve.wait_ge(m["w_in"], 32)
            chain(dve.tensor_tensor(E[:], E[:], over(s[:], tiles), ALU.mult))
            dve.wait_ge(m["root_ready"], 1)
            chain(dve.reciprocal(var[:], var[:]))
            chain(dve.tensor_tensor(E[:], E[:], each(var[:], D), ALU.mult))
            chain(dve.tensor_tensor(E[:], E[:], over(b[:], tiles), ALU.add))

        @block.scalar
        def _(act):
            act.wait_ge(m["var_ready"], 1)
            act.activation(var[:], var[:], ACT.Sqrt, scale=1.0 / D, bias=c.eps6[0:NODE_TILE, :])\
                .then_inc(m["root_ready"], 1)


def gnn_out(nc, c, ins, E, X):
    tiles = E.shape[1]
    with ExitStack() as st:
        def sb(n, shape, dt=F32):
            return st.enter_context(nc.sbuf_tensor(f"inv_{n}", shape, dt))

        def psum(n):
            return [st.enter_context(nc.psum_tensor(f"inv_{n}{h}", [LANES, 512], F32)) for h in range(2)]

        w = sb("w", [D, GIN])
        b = sb("b", [NODE_TILE, GIN])
        E_tile = sb("E_tile", [NODE_TILE, 2, D])
        ET = sb("ET", [D, 2, NODE_TILE])
        ps_t, ps_x = psum("ps_t"), psum("ps_x")
        m = sem_set(nc, st, "inv", ["w_in", "taken", "turned", "turned_sb", "projected", "added", "chain"])
        block = st.enter_context(nc.Block())

        @block.sync
        def _(sp):
            sp.dma_start(w[:], ins["L0_gnn_inv_w"]).then_inc(m["w_in"], 16)
            load_row(sp, b[:], ins["L0_gnn_inv_b"], m["w_in"])

        @block.tensor
        def _(pe):
            pe.wait_ge(m["w_in"], 32)

            def turn(t, r, h):
                pe.wait_ge(m["taken"], t + 1)
                wait(pe, m["turned_sb"], t - 1)
                pe.transpose(ps_t[h][:, 0:NODE_TILE], E_tile[:, h, :], c.ident[0:NODE_TILE, 0:NODE_TILE])\
                    .then_inc(m["turned"], 1)

            def times_w(t, r, h):
                pe.wait_ge(m["turned_sb"], t + 1)
                wait(pe, m["added"], t - 1)
                pe.matmul(ps_x[h][0:NODE_TILE, 0:GIN], ET[:, h, :], w[:], start=True, stop=True)\
                    .then_inc(m["projected"], 1)
            node_steps(pe, tiles, [(1, times_w), (2, turn)])

        @block.scalar
        def _(act):
            def take(t, r, h):
                wait(act, m["turned"], t - 1)
                act.nop(nofuse=True)
                act.copy(E_tile[:, h, :], at(E, t)).then_inc(m["taken"], 1)

            def copy_turned(t, r, h):
                act.wait_ge(m["turned"], t + 1)
                wait(act, m["projected"], t - 1)
                act.copy(ET[:, h, :], ps_t[h][:, 0:NODE_TILE]).then_inc(m["turned_sb"], 1)
            node_steps(act, tiles, [(2, copy_turned), (3, take)])

        @block.vector
        def _(dve):
            dve.wait_ge(m["w_in"], 32)
            chain = Chain(dve, m["chain"])
            chain(dve.tensor_tensor(X[:], X[:], over(b[:], tiles), ALU.add))

            def add(t, r, h):
                dve.wait_ge(m["projected"], t + 1)
                dve.tensor_tensor(at(X, t), at(X, t), ps_x[h][0:NODE_TILE, 0:GIN], ALU.add).then_inc(m["added"], 1)
            node_steps(dve, tiles, [(0, add)])


FH, EXPERTS = 4, 4
FE = FH * EXPERTS
SPLIT = 3
ROW = FE + FH + SPLIT * FH // 2


def split3(dve, chain, parts, value, rest):
    chain(dve.tensor_copy(parts[0], value))
    chain(dve.tensor_tensor(rest, value, parts[0], ALU.subtract))
    chain(dve.tensor_copy(parts[1], rest))
    chain(dve.tensor_tensor(parts[2], rest, parts[1], ALU.subtract))


def router_rows(nc, c, ins, X, mean, rstd, row, a_dst, table):
    tiles = X.shape[1]
    with ExitStack() as st:
        def sb(n, shape, dt=F32):
            return st.enter_context(nc.sbuf_tensor(f"row_{n}", shape, dt))

        def psum(n):
            return [st.enter_context(nc.psum_tensor(f"row_{n}{h}", [LANES, 512], F32)) for h in range(2)]

        w = sb("w", [LANES, KC, FE])
        att = sb("att", [NODE_TILE, 2, FE])
        xn = sb("xn", [NODE_TILE, 2, GIN])
        xT = sb("xT", [LANES, 2, KC, NODE_TILE])
        tmp = sb("tmp", [NODE_TILE, tiles, FE])
        rest = sb("rest", [NODE_TILE, tiles, FH])
        ps_t, ps_h = psum("ps_t"), psum("ps_h")
        m = sem_set(nc, st, "row", ["w_in", "normed", "turned", "turned_sb", "projected", "h_out", "chain", "rows",
                                    "stored"])
        block = st.enter_context(nc.Block())

        @block.sync
        def _(sp):
            sp.dma_start(w[:], ins["L0_ffn_W_gat"].rearrange("(c p) n -> p c n", p=LANES)).then_inc(m["w_in"], 16)
            load_row(sp, att[:, 0, :], ins["L0_ffn_att_src"].rearrange("a b -> (a b)"), m["w_in"])
            load_row(sp, att[:, 1, :], ins["L0_ffn_att_dst"].rearrange("a b -> (a b)"), m["w_in"])
            sp.wait_ge(m["rows"], 1)
            sp.dma_start(table.rearrange(TILE_ROWS, p=NODE_TILE), row[:]).then_inc(m["stored"], 16)
            sp.wait_ge(m["stored"], 16)

        @block.tensor
        def _(pe):
            pe.wait_ge(m["w_in"], 48)

            def turn(t, r, h):
                pe.wait_ge(m["normed"], t + 1)
                wait(pe, m["turned_sb"], t - 1)
                for ch in range(KC):
                    ins = pe.transpose(ps_t[h][:, ch * NODE_TILE:(ch + 1) * NODE_TILE],
                                       xn[:, h, ch * LANES:(ch + 1) * LANES], c.ident[0:NODE_TILE, 0:NODE_TILE])
                ins.then_inc(m["turned"], 1)

            def times_w(t, r, h):
                pe.wait_ge(m["turned_sb"], t + 1)
                wait(pe, m["h_out"], t - 1)
                for ch in range(KC):
                    ins = pe.matmul(ps_h[h][0:NODE_TILE, 0:FE], xT[:, h, ch, :], w[:, ch, :], start=ch == 0,
                                    stop=ch == KC - 1)
                ins.then_inc(m["projected"], 1)
            node_steps(pe, tiles, [(0, times_w), (1, turn)])

        @block.scalar
        def _(act):
            def copy_turned(t, r, h):
                act.wait_ge(m["turned"], t + 1)
                wait(act, m["projected"], t - 1)
                act.copy(xT[:, h], ps_t[h][:, 0:KC * NODE_TILE].rearrange("p (c n) -> p c n", c=KC))\
                    .then_inc(m["turned_sb"], 1)
            node_steps(act, tiles, [(0, copy_turned)])

        @block.vector
        def _(dve):
            def norm(t, r, h):
                wait(dve, m["turned"], t - 1)
                dve.tensor_scalar(xn[:, h, :], at(X, t), at2(mean, t), at2(rstd, t), ALU.subtract, ALU.mult)\
                    .then_inc(m["normed"], 1)

            def h_out(t, r, h):
                dve.wait_ge(m["projected"], t + 1)
                dve.tensor_copy(at(row, t)[:, 0:FE], ps_h[h][0:NODE_TILE, 0:FE]).then_inc(m["h_out"], 1)
            node_steps(dve, tiles, [(2, norm), (0, h_out)])
            dve.wait_ge(m["h_out"], tiles)
            dve.wait_ge(m["w_in"], 48)
            chain = Chain(dve, m["chain"])
            for n, sums in ((0, row[:, :, FE:FE + FH]), (1, a_dst[:])):
                chain(dve.tensor_tensor(tmp[:], row[:, :, 0:FE], over(att[:, n, :], tiles), ALU.mult))
                chain(dve.tensor_reduce(sums, tmp[:].rearrange("p t (h e) -> p t h e", e=EXPERTS), AX, ALU.add))
            parts = row[:, :, FE + FH:ROW].bitcast(BF16)
            split3(dve, chain, [parts[:, :, n * FH:(n + 1) * FH] for n in range(SPLIT)], row[:, :, FE:FE + FH], rest[:])
            dve.tensor_copy(tmp[:, 0:1, 0:1], rest[:, 0:1, 0:1]).then_inc(m["rows"], 1)


def neighbour_max(nc, c, g, table, best, src_sb):
    with ExitStack() as st:
        def sb(n, shape, dt=F32):
            return st.enter_context(nc.sbuf_tensor(f"max_{n}", shape, dt))

        def psum(n, count, dt=F32):
            return [st.enter_context(nc.psum_tensor(f"max_{n}{h}", [LANES, 2048 // (4 if dt == F32 else 2)], dt))
                    for h in range(count)]

        stage = sb("stage", [LANES, SLOTS, GROUP, 2], I32)
        rows = sb("rows", [LANES, SLOTS, GROUP, ROW])
        hot = sb("hot", [LANES, 2, GROUP, NODE_TILE])
        far = sb("far", [NODE_TILE, 2, GROUP * LANES])
        a_t = sb("a_t", [SPLIT * FH, 2, GROUP * LANES], BF16)
        junk = sb("junk", [NODE_TILE, 2, 8, PAIR * LANES], BF16)
        top = sb("top", [NODE_TILE, 2, GROUP // PAIR, FH])
        tile_of = sb("tile_of", [1, g.pairs], I32)
        minus_far = sb("minus_far", [LANES, 1])
        ps_hot, ps_a = psum("ps_hot", 2), psum("ps_a", 2, BF16)
        ps_b = psum("ps_b", 4)
        m = sem_set(nc, st, "max", ["tiles_in", "one_hots", "turned", "turned_sb", "a_turned", "a_sb", "kept",
                                    "tops", "maxed", "started"] + [f"spread{n}" for n in range(4)] +
                    [f"topped{n}" for n in range(4)])
        spread = [m["spread0"], m["spread1"], m["spread2"], m["spread3"]]
        topped = [m["topped0"], m["topped1"], m["topped2"], m["topped3"]]
        m["staged"] = st.enter_context(semaphores(nc, [f"max_staged{j}" for j in range(SLOTS)]))
        m["gathered"] = c.gathered["max"]
        total = g.edge_tiles // GROUP
        block = st.enter_context(nc.Block())

        @block.sync
        def _(sp):
            sp.dma_start(tile_of[:], g.pair_tile.rearrange("(a n) -> a n", a=1)).then_inc(m["tiles_in"], 16)
            stage_slots(sp, g, stage, m, m["gathered"])

        @block.gpsimd
        def _(pool):
            gather_rows(pool, g, stage, lambda k, j, e: rows[:, j, e, :], table, m, used=m["a_turned"], also=m["kept"])

        @block.tensor
        def _(pe):
            def turn(k, r, j):
                pe.wait_ge(m["one_hots"], k + 1)
                wait(pe, m["turned_sb"], k - 1)
                for e in range(GROUP):
                    ins = pe.transpose(ps_hot[j % 2][0:NODE_TILE, e * LANES:(e + 1) * LANES], hot[:, j % 2, e, :],
                                       c.ident[:])
                ins.then_inc(m["turned"], 1)

            def turn_a(k, r, j):
                pe.wait_ge(m["gathered"][j], (r + 1) * (16 * GROUP))
                wait(pe, m["a_sb"], k - 1)
                for e in range(GROUP):
                    ins = pe.transpose(ps_a[j % 2][0:SPLIT * FH, e * LANES:(e + 1) * LANES],
                                       rows[:, j, e, FE + FH:ROW].bitcast(BF16), c.ident16[:])
                ins.then_inc(m["a_turned"], 1)

            def spread_a(k, r, j):
                pe.wait_ge(m["a_sb"], k + 1)
                for n in range(4):
                    wait(pe, topped[n], k)
                    for i in range(2):
                        head = n % 2 * 2 + i
                        ins = pe.matmul(ps_b[n][0:NODE_TILE, i * 256:(i + 1) * 256], c.pick_head[:, head, :],
                                        a_t[:, j % 2, n // 2 * 256:(n // 2 + 1) * 256], start=True, stop=True)
                    ins.then_inc(spread[n], 1)
            edge_steps(pe, total, [(0, spread_a), (1, turn), (1, turn_a)])

        @block.scalar
        def _(act):
            act.wait_ge(m["started"], 1)

            def copy_a(k, r, j):
                act.wait_ge(m["a_turned"], k + 1)
                wait(act, m["spread3"], k - 1)
                act.copy(a_t[:, j % 2, :], ps_a[j % 2][0:SPLIT * FH, 0:GROUP * LANES]).then_inc(m["a_sb"], 1)

            def copy_turned(k, r, j):
                act.wait_ge(m["turned"], k + 1)
                wait(act, m["topped3"], k - 1)
                act.activation(far[:, j % 2, :], ps_hot[j % 2][0:NODE_TILE, :], ACT.Identity, scale=1e30,
                               bias=minus_far[0:NODE_TILE, :]).then_inc(m["turned_sb"], 1)

            def keep(k, r, j):
                act.wait_ge(m["gathered"][j], (r + 1) * (16 * GROUP))
                act.nop(nofuse=True)
                act.copy(src_sb[:, bass.ds(k * GROUP, GROUP), :], rows[:, j, :, 0:FE + FH]).then_inc(m["kept"], 1)
            edge_steps(act, total, [(1, copy_a), (1, copy_turned), (0, keep)])

        @block.vector
        def _(dve):
            dve.memset(minus_far[:], -1e30).then_inc(m["started"], 1)
            dve.wait_ge(m["tiles_in"], 16)

            def one_hot(k, r, j):
                dve.wait_ge(m["staged"][j], (r + 1) * 16)
                wait(dve, m["turned"], k - 1)
                dve.tensor_tensor(hot[:, j % 2], c.node_no[:],
                                  stage[:, j, :, 1:2].broadcast_to([LANES, GROUP, NODE_TILE]), ALU.is_equal)\
                    .then_inc(m["one_hots"], 1)

            def tops(k, r, j):
                dve.wait_ge(m["turned_sb"], k + 1)
                wait(dve, m["maxed"], 2 * (k - 2) + 2)
                for n in range(4):
                    dve.wait_ge(spread[n], k + 1)
                    dve.nop(nofuse=True)
                    for i in range(2):
                        head = n % 2 * 2 + i
                        ins = dve.tensor_tensor_reduce(
                            out=junk[:, j % 2, 2 * n + i, :], in0=far[:, j % 2, n // 2 * 256:(n // 2 + 1) * 256],
                            in1=ps_b[n][0:NODE_TILE, i * 256:(i + 1) * 256], scale=1.0, scalar=-1e30,
                            op0=ALU.add, op1=ALU.max, accum_out=top[:, j % 2, n // 2, head:head + 1])
                    ins.then_inc(topped[n], 1)

            def maxes(k, r, j):
                dve.wait_ge(m["topped3"], k + 1)
                for p in range(GROUP // PAIR):
                    t = dve.value_load(tile_of[0:1, bass.ds(k * (GROUP // PAIR) + p, 1)], min_val=0,
                                       max_val=g.tiles - 1)
                    wait(dve, m["maxed"], 2 * k + p)
                    dve.tensor_tensor(at(best, t), at(best, t), top[:, j % 2, p, :], ALU.max).then_inc(m["maxed"], 1)
            edge_steps(dve, total, [(2, one_hot), (0, tops), (-1, maxes)])


def router_weights(nc, c, row, a_dst, best, node_info, gacc):
    tiles = row.shape[1]
    with ExitStack() as st:
        def sb(n, shape):
            return st.enter_context(nc.sbuf_tensor(f"self_{n}", shape, F32))

        info = sb("info", [NODE_TILE, tiles, 2 * FH])
        rest = sb("rest", [NODE_TILE, tiles, 2 * FH])
        own = sb("own", [NODE_TILE, tiles, FH])
        m = sem_set(nc, st, "self", ["chain", "own_ready", "exp_ready"])
        block = st.enter_context(nc.Block())

        @block.vector
        def _(dve):
            chain = Chain(dve, m["chain"])
            top = info[:, :, FH:2 * FH]
            chain(dve.tensor_tensor(top, best[:], a_dst[:], ALU.add))
            chain(dve.scalar_tensor_tensor(out=top, in0=top, scalar=0.2, in1=top, op0=ALU.mult, op1=ALU.max))
            chain(dve.tensor_tensor(own[:], row[:, :, FE:FE + FH], a_dst[:], ALU.add))
            chain(dve.scalar_tensor_tensor(out=own[:], in0=own[:], scalar=0.2, in1=own[:], op0=ALU.mult, op1=ALU.max))
            dve.tensor_tensor(own[:], own[:], top, ALU.subtract).then_inc(m["own_ready"], 1)
            chain(dve.tensor_copy(info[:, :, 0:FH], a_dst[:]))
            split3(dve, chain, [node_info[:, :, n, :] for n in range(SPLIT)], info[:], rest[:])
            dve.wait_ge(m["exp_ready"], 1)
            for h in range(FH):
                last = dve.tensor_tensor(gacc[:, :, h * EXPERTS:(h + 1) * EXPERTS],
                                         row[:, :, h * EXPERTS:(h + 1) * EXPERTS],
                                         gacc[:, :, FE + h:FE + h + 1].broadcast_to([NODE_TILE, tiles, EXPERTS]), ALU.mult)
            chain(last)

        @block.scalar
        def _(act):
            act.wait_ge(m["own_ready"], 1)
            act.activation(gacc[:, :, FE:FE + FH], own[:], ACT.Exp).then_inc(m["exp_ready"], 1)


def neighbour_sum(nc, c, g, src_sb, node_info, gacc):
    with ExitStack() as st:
        def sb(n, shape, dt=F32):
            return st.enter_context(nc.sbuf_tensor(f"gs_{n}", shape, dt))

        def psum(n):
            return [st.enter_context(nc.psum_tensor(f"gs_{n}{h}", [LANES, 512], F32)) for h in range(2)]

        stage = sb("stage", [LANES, SLOTS, GROUP, 2], I32)
        hot = sb("hot", [LANES, SLOTS, GROUP, NODE_TILE])
        hot_t = sb("hot_t", [NODE_TILE, 2, GROUP * LANES], BF16)
        e_sb = sb("e_sb", [LANES, 2, GROUP, FH])
        vals = sb("vals", [LANES, 2, GROUP, FE + FH])
        tile_of = sb("tile_of", [1, g.pairs], I32)
        ps_hot, ps_n, ps_sum = psum("ps_hot"), psum("ps_n"), psum("ps_sum")
        m = sem_set(nc, st, "gs", ["tiles_in", "one_hots", "turned", "turned_sb", "info", "sums", "leaky", "less",
                                   "exps", "weighted", "summed", "added"])
        m["staged"] = st.enter_context(semaphores(nc, [f"gs_staged{j}" for j in range(SLOTS)]))
        total = g.edge_tiles // GROUP
        block = st.enter_context(nc.Block())

        def node_tile(eng, pair):
            return eng.value_load(tile_of[0:1, bass.ds(pair, 1)], min_val=0, max_val=g.tiles - 1)

        @block.sync
        def _(sp):
            sp.dma_start(tile_of[:], g.pair_tile.rearrange("(a n) -> a n", a=1)).then_inc(m["tiles_in"], 16)
            stage_slots(sp, g, stage, m)

        @block.tensor
        def _(pe):
            pe.wait_ge(m["tiles_in"], 16)

            def turn(k, r, j):
                pe.wait_ge(m["one_hots"], k + 1)
                wait(pe, m["turned_sb"], k - 1)
                for e in range(GROUP):
                    ins = pe.transpose(ps_hot[j % 2][0:NODE_TILE, e * LANES:(e + 1) * LANES], hot[:, j, e, :],
                                       c.ident[:])
                ins.then_inc(m["turned"], 1)

            def fetch(k, r, j):
                pe.wait_ge(m["turned_sb"], k + 1)
                wait(pe, m["less"], k - 1)
                for p in range(GROUP // PAIR):
                    t = node_tile(pe, k * (GROUP // PAIR) + p)
                    for e in range(PAIR * p, PAIR * (p + 1)):
                        for n in range(SPLIT):
                            ins = pe.matmul(ps_n[j % 2][:, e * 2 * FH:(e + 1) * 2 * FH],
                                            hot_t[:, j % 2, e * LANES:(e + 1) * LANES], at(node_info, t)[:, n, :],
                                            start=n == 0, stop=n == SPLIT - 1)
                ins.then_inc(m["info"], 1)

            def add_up(k, r, j):
                pe.wait_ge(m["weighted"], k + 1)
                wait(pe, m["added"], 2 * (k - 2) + 2)
                for p in range(GROUP // PAIR):
                    for e in range(PAIR):
                        ins = pe.matmul(ps_sum[j % 2][0:NODE_TILE, p * 256:p * 256 + FE + FH],
                                        hot[:, j, PAIR * p + e, :], vals[:, j % 2, PAIR * p + e, :],
                                        start=e == 0, stop=e == PAIR - 1)
                ins.then_inc(m["summed"], 1)
            edge_steps(pe, total, [(-2, add_up), (1, fetch), (2, turn)])

        @block.scalar
        def _(act):
            def copy_turned(k, r, j):
                act.wait_ge(m["turned"], k + 1)
                wait(act, m["info"], k - 1)
                act.copy(hot_t[:, j % 2, :], ps_hot[j % 2][0:NODE_TILE, :]).then_inc(m["turned_sb"], 1)

            def exps(k, r, j):
                act.wait_ge(m["less"], k + 1)
                wait(act, m["summed"], k - 1)
                act.activation(vals[:, j % 2, :, FE:FE + FH], e_sb[:, j % 2], ACT.Exp).then_inc(m["exps"], 1)
            edge_steps(act, total, [(2, copy_turned), (0, exps)])

        @block.vector
        def _(dve):
            dve.wait_ge(m["tiles_in"], 16)

            def src_of(k):
                return src_sb[:, bass.ds(k * GROUP, GROUP), :]

            def sums(k, r, j):
                dve.wait_ge(m["info"], k + 1)
                wait(dve, m["exps"], k - 1)
                info = ps_n[j % 2][:, 0:GROUP * 2 * FH].rearrange("p (e f) -> p e f", e=GROUP)
                dve.tensor_tensor(e_sb[:, j % 2], src_of(k)[:, :, FE:FE + FH], info[:, :, 0:FH], ALU.add)\
                    .then_inc(m["sums"], 1)

            def one_hot(k, r, j):
                dve.wait_ge(m["staged"][j], (r + 1) * 16)
                wait(dve, m["summed"], (k - SLOTS) + 1)
                dve.tensor_tensor(hot[:, j], c.node_no[:],
                                  stage[:, j, :, 1:2].broadcast_to([LANES, GROUP, NODE_TILE]), ALU.is_equal)\
                    .then_inc(m["one_hots"], 1)

            def leaky(k, r, j):
                dve.wait_ge(m["sums"], k + 1)
                dve.scalar_tensor_tensor(out=e_sb[:, j % 2], in0=e_sb[:, j % 2], scalar=0.2, in1=e_sb[:, j % 2],
                                         op0=ALU.mult, op1=ALU.max).then_inc(m["leaky"], 1)

            def less(k, r, j):
                dve.wait_ge(m["leaky"], k + 1)
                info = ps_n[j % 2][:, 0:GROUP * 2 * FH].rearrange("p (e f) -> p e f", e=GROUP)
                dve.tensor_tensor(e_sb[:, j % 2], e_sb[:, j % 2], info[:, :, FH:2 * FH], ALU.subtract)\
                    .then_inc(m["less"], 1)

            def weigh(k, r, j):
                dve.wait_ge(m["exps"], k + 1)
                for h in range(FH):
                    ins = dve.tensor_tensor(
                        vals[:, j % 2, :, h * EXPERTS:(h + 1) * EXPERTS],
                        src_of(k)[:, :, h * EXPERTS:(h + 1) * EXPERTS],
                        vals[:, j % 2, :, FE + h:FE + h + 1].broadcast_to([LANES, GROUP, EXPERTS]), ALU.mult)
                ins.then_inc(m["weighted"], 1)

            def add_sums(k, r, j):
                dve.wait_ge(m["summed"], k + 1)
                for p in range(GROUP // PAIR):
                    t = node_tile(dve, k * (GROUP // PAIR) + p)
                    wait(dve, m["added"], 2 * k + p)
                    dve.tensor_tensor(at(gacc, t), at(gacc, t), ps_sum[j % 2][0:NODE_TILE, p * 256:p * 256 + FE + FH],
                                      ALU.add).then_inc(m["added"], 1)
            edge_steps(dve, total, [(0, sums), (-1, weigh), (0, leaky), (2, one_hot), (0, less), (-2, add_sums)])


def gates(nc, c, ins, gacc, gate):
    tiles = gacc.shape[1]
    with ExitStack() as st:
        def sb(n, shape):
            return st.enter_context(nc.sbuf_tensor(f"gate_{n}", shape, F32))

        par = sb("par", [NODE_TILE, 3, FE])
        agg = sb("agg", [NODE_TILE, tiles, FE])
        sq = sb("sq", [NODE_TILE, tiles, FE])
        mean, var = sb("mean", [NODE_TILE, tiles]), sb("var", [NODE_TILE, tiles])
        score = sb("score", [NODE_TILE, tiles, EXPERTS])
        better = sb("better", [NODE_TILE, tiles, EXPERTS])
        beats = sb("beats", [NODE_TILE, tiles, 1])
        m = sem_set(nc, st, "gate", ["w_in", "chain", "var_ready", "root_ready", "exp_in", "exp_ready"])
        block = st.enter_context(nc.Block())

        @block.sync
        def _(sp):
            for n, name in enumerate(("L0_ffn_b_gat", "L0_ffn_ln_gamma", "L0_ffn_ln_beta")):
                load_row(sp, par[:, n, :], ins[name], m["w_in"])

        @block.scalar
        def _(act):
            act.wait_ge(m["var_ready"], 1)
            act.activation(var[:], var[:], ACT.Sqrt, scale=1.0 / FE, bias=c.eps5[0:NODE_TILE, :])\
                .then_inc(m["root_ready"], 1)
            act.wait_ge(m["exp_in"], 1)
            act.activation(score[:], score[:], ACT.Exp).then_inc(m["exp_ready"], 1)

        @block.vector
        def _(dve):
            chain = Chain(dve, m["chain"])
            dens = gacc[:, :, FE:FE + FH]
            chain(dve.tensor_scalar(dens, dens, 1e-16, None, ALU.add))
            chain(dve.reciprocal(dens, dens))
            for h in range(FH):
                last = dve.tensor_tensor(agg[:, :, h * EXPERTS:(h + 1) * EXPERTS],
                                         gacc[:, :, h * EXPERTS:(h + 1) * EXPERTS],
                                         gacc[:, :, FE + h:FE + h + 1].broadcast_to([NODE_TILE, tiles, EXPERTS]), ALU.mult)
            chain(last)
            dve.wait_ge(m["w_in"], 48)
            chain(dve.tensor_tensor(agg[:], agg[:], over(par[:, 0, :], tiles), ALU.add))
            chain(dve.tensor_reduce(mean[:], agg[:], AX, ALU.add))
            chain(dve.tensor_scalar(mean[:], mean[:], 1.0 / FE, None, ALU.mult))
            chain(dve.tensor_tensor(agg[:], agg[:], each(mean[:], FE), ALU.subtract))
            chain(dve.tensor_tensor(sq[:], agg[:], agg[:], ALU.mult))
            dve.tensor_reduce(var[:], sq[:], AX, ALU.add).then_inc(m["var_ready"], 1)
            dve.wait_ge(m["root_ready"], 1)
            chain(dve.reciprocal(var[:], var[:]))
            chain(dve.tensor_tensor(agg[:], agg[:], each(var[:], FE), ALU.mult))
            chain(dve.tensor_tensor(agg[:], agg[:], over(par[:, 1, :], tiles), ALU.mult))
            chain(dve.tensor_tensor(agg[:], agg[:], over(par[:, 2, :], tiles), ALU.add))
            chain(dve.tensor_tensor(score[:], agg[:, :, 0:EXPERTS], agg[:, :, EXPERTS:2 * EXPERTS], ALU.add))
            for h in range(2, FH):
                chain(dve.tensor_tensor(score[:], score[:], agg[:, :, h * EXPERTS:(h + 1) * EXPERTS], ALU.add))
            chain(dve.tensor_scalar(score[:], score[:], 1.0 / FH, None, ALU.mult))
            chain(dve.memset(better[:], 0.0))
            for i in range(EXPERTS):
                for j in range(EXPERTS):
                    if i != j:
                        chain(dve.tensor_tensor(beats[:], score[:, :, j:j + 1], score[:, :, i:i + 1],
                                                ALU.is_ge if j < i else ALU.is_gt))
                        chain(dve.tensor_tensor(better[:, :, i:i + 1], better[:, :, i:i + 1], beats[:], ALU.add))
            chain(dve.tensor_scalar(better[:], better[:], 2.0, None, ALU.is_lt))
            chain(dve.tensor_reduce(mean[:], score[:], AX, ALU.max))
            dve.tensor_tensor(score[:], score[:], each(mean[:], EXPERTS), ALU.subtract).then_inc(m["exp_in"], 1)
            dve.wait_ge(m["exp_ready"], 1)
            chain(dve.tensor_tensor(score[:], score[:], better[:], ALU.mult))
            chain(dve.tensor_reduce(mean[:], score[:], AX, ALU.add))
            chain(dve.reciprocal(mean[:], mean[:]))
            chain(dve.tensor_tensor(gate[:], score[:], each(mean[:], EXPERTS), ALU.mult))


HIDDEN = 512
HC = HIDDEN // LANES
TWO = 2 * NODE_TILE


def experts(nc, c, ins, X, mean, rstd, gate):
    tiles = X.shape[1]
    with ExitStack() as st:
        def sb(n, shape, dt=F32):
            return st.enter_context(nc.sbuf_tensor(f"ex_{n}", shape, dt))

        def psum(n, count=2):
            return [st.enter_context(nc.psum_tensor(f"ex_{n}{h}", [LANES, 512], F32)) for h in range(count)]

        w1 = sb("w1", [LANES, EXPERTS, KC, HIDDEN])
        w2 = sb("w2", [LANES, EXPERTS, HC, GIN])
        b1 = sb("b1", [LANES, EXPERTS, HC])
        b2 = sb("b2", [NODE_TILE, EXPERTS, GIN])
        xn = sb("xn", [NODE_TILE, 2, 2, GIN])
        xT = sb("xT", [LANES, 2, KC, TWO])
        hid = sb("hid", [LANES, 2, HC, TWO])
        ps_t, ps_h, ps_o = psum("ps_t"), psum("ps_h", 4), psum("ps_o")
        m = sem_set(nc, st, "ex", ["w_in", "normed", "turned", "turned_sb", "gelus", "hidden", "summed", "added",
                              "biased"])
        block = st.enter_context(nc.Block())
        steps = tiles // 2

        @block.sync
        def _(sp):
            sp.dma_start(w1[:], ins["L0_ffn_W1"].rearrange("e (c p) n -> p e c n", p=LANES)).then_inc(m["w_in"], 16)
            sp.dma_start(w2[:], ins["L0_ffn_W2"].rearrange("e (c p) n -> p e c n", p=LANES)).then_inc(m["w_in"], 16)
            for e in range(EXPERTS):
                sp.dma_start(b1[:, e, :], ins["L0_ffn_b1"][e].rearrange("(c p) -> p c", p=LANES),
                             allow_slow_non_contiguous=True).then_inc(m["w_in"], 16)
                load_row(sp, b2[:, e, :], ins["L0_ffn_b2"][e], m["w_in"])

        loads = 16 * (2 + 2 * EXPERTS)

        @block.tensor
        def _(pe):
            pe.wait_ge(m["w_in"], loads)

            def turn(t, r, h):
                pe.wait_ge(m["normed"], t + 1)
                wait(pe, m["turned_sb"], t - 1)
                for ch in range(KC):
                    for n in range(2):
                        a = ch * TWO + n * NODE_TILE
                        ins = pe.transpose(ps_t[h][:, a:a + NODE_TILE], xn[:, h, n, ch * LANES:(ch + 1) * LANES],
                                           c.ident[0:NODE_TILE, 0:NODE_TILE])
                ins.then_inc(m["turned"], 1)

            def step(t, r, h):
                pe.wait_ge(m["turned_sb"], t + 1)

                def hidden(e):
                    for b in range(2):
                        wait(pe, m["gelus"], (t * EXPERTS + e - 2) * 2 + b + 1)
                        for i in range(2):
                            for ch in range(KC):
                                a = (2 * b + i) * LANES
                                ins = pe.matmul(ps_h[e % 2 * 2 + b][:, i * TWO:(i + 1) * TWO],
                                                w1[:, e, ch, a:a + LANES], xT[:, h, ch, :], start=ch == 0,
                                                stop=ch == KC - 1)
                        ins.then_inc(m["hidden"], 1)

                def outs(e):
                    pe.wait_ge(m["gelus"], (t * EXPERTS + e) * 2 + 2)
                    for n in range(2):
                        wait(pe, m["added"], (t * EXPERTS + e) * 2 + n - 1)
                        for hc in range(HC):
                            ins = pe.matmul(ps_o[n][0:NODE_TILE, 0:GIN], hid[:, e % 2, hc, n * NODE_TILE:(n + 1) * NODE_TILE],
                                      w2[:, e, hc, :], start=hc == 0, stop=hc == HC - 1)
                        ins.then_inc(m["summed"], 1)
                hidden(0)
                for e in range(EXPERTS):
                    if e + 1 < EXPERTS:
                        hidden(e + 1)
                    outs(e)
            node_steps(pe, steps, [(1, turn), (0, step)])

        @block.scalar
        def _(act):
            act.wait_ge(m["w_in"], loads)

            def copy_turned(t, r, h):
                act.wait_ge(m["turned"], t + 1)
                wait(act, m["summed"], (t - 1) * EXPERTS * 2)
                act.copy(xT[:, h], ps_t[h][:, 0:KC * TWO].rearrange("p (c n) -> p c n", c=KC)).then_inc(m["turned_sb"], 1)

            def gelu(t, r, h):
                for e in range(EXPERTS):
                    wait(act, m["summed"], (t * EXPERTS + e - 1) * 2)
                    for b in range(2):
                        act.wait_ge(m["hidden"], (t * EXPERTS + e) * 2 + b + 1)
                        for i in range(2):
                            ins = act.activation(hid[:, e % 2, 2 * b + i, :], ps_h[e % 2 * 2 + b][:, i * TWO:(i + 1) * TWO],
                                                 ACT.Gelu, bias=b1[:, e, 2 * b + i:2 * b + i + 1])
                        ins.then_inc(m["gelus"], 1)
            node_steps(act, steps, [(1, copy_turned), (0, gelu)])

        @block.vector
        def _(dve):
            def norm(t, r, h):
                wait(dve, m["turned"], t - 1)
                for n in range(2):
                    ins = dve.tensor_scalar(xn[:, h, n, :], at(X, t * 2 + n), at2(mean, t * 2 + n), at2(rstd, t * 2 + n),
                                            ALU.subtract, ALU.mult)
                ins.then_inc(m["normed"], 1)

            def add(t, r, h):
                for e in range(EXPERTS):
                    for n in range(2):
                        done = (t * EXPERTS + e) * 2 + n
                        dve.wait_ge(m["summed"], done + 1)
                        wait(dve, m["added"], done - 1)
                        x = at(X, t * 2 + n)
                        dve.scalar_tensor_tensor(out=x, in0=ps_o[n][0:NODE_TILE, 0:GIN],
                                                 scalar=at(gate, t * 2 + n)[:, e:e + 1], in1=x, op0=ALU.mult, op1=ALU.add)\
                            .then_inc(m["added"], 1)

            def bias(t, r, h):
                for n in range(2):
                    x = at(X, t * 2 + n)
                    dve.wait_ge(m["added"], ((t * EXPERTS) + EXPERTS - 1) * 2 + n + 1)
                    for e in range(EXPERTS):
                        wait(dve, m["biased"], (t * 2 + n) * EXPERTS + e)
                        dve.scalar_tensor_tensor(out=x, in0=b2[:, e, :], scalar=at(gate, t * 2 + n)[:, e:e + 1], in1=x,
                                                 op0=ALU.mult, op1=ALU.add).then_inc(m["biased"], 1)
            dve.wait_ge(m["w_in"], loads)
            node_steps(dve, steps, [(2, norm), (0, add), (0, bias)])


def program(nc, ins, out):
    with ExitStack() as ctx:
        moved = {n: [ctx.enter_context(nc.semaphore(f"{n}_moved{h}")) for h in range(2)] for n in ("gnn", "gat")}
        gathered = {n: [ctx.enter_context(nc.semaphore(f"{n}_gathered{j}")) for j in range(SLOTS)]
                    for n in ("att1", "att2", "max")}
        c = constants(nc, ctx)
        c.moved, c.gathered = moved, gathered
        gnn = Graph(nc, "gnn", ins["src"], ins["dst"], 200000, 125, 6250, 6250)
        ei = ins["L0_ffn_edge_index"]
        gat = Graph(nc, "gat", ei[1], ei[0], 131072, 128, 6250, 8192)
        tiles = gnn.tiles
        kv = nc.dram_tensor("kv", [gnn.nodes, 2 * D], F32, kind="Internal").ap()
        rows = nc.dram_tensor("rows", [gnn.nodes, ROW], F32, kind="Internal").ap()
        place(nc, c, (gnn, gat))

        def sb(stack, name, shape, dt=F32):
            return stack.enter_context(nc.sbuf_tensor(name, shape, dt))
        X = sb(ctx, "X", [NODE_TILE, tiles, GIN])
        mean, var, rstd = (sb(ctx, n, [NODE_TILE, tiles]) for n in ("mean", "var", "rstd"))
        with ExitStack() as gs:
            E = sb(gs, "E", [NODE_TILE, tiles, D])
            row_statistics(nc, c, "stat1", X, GIN, mean, rstd, var, c.eps5,
                           source=ins["x"].rearrange(TILE_ROWS, p=NODE_TILE))
            with ExitStack() as ms:
                mean_rstd, mix_rstd = (sb(ms, n, [NODE_TILE, tiles]) for n in ("mean_rstd", "mix_rstd"))
                key_values = sb(ms, "key_values", [LANES, KC, LANES])
                key_sums = sb(ms, "key_sums", [LANES, KC, LANES])
                mix_scales(nc, c, mean, rstd, var, mean_rstd, mix_rstd)
                embed(nc, c, ins, X, mean, rstd, mix_rstd, E, key_values, key_sums)
                H = sb(ms, "H", [NODE_TILE, tiles, GIN])
                mix(nc, c, ins, X, mean, rstd, mean_rstd, mix_rstd, key_values, key_sums, H)
                tmp = sb(ms, "tmp", [NODE_TILE, tiles, GIN])
                mix_finish(nc, c, ins, X, H, tmp)
            for n in "12":
                with ExitStack() as ls:
                    acc = sb(ls, f"acc{n}", [NODE_TILE, tiles, SUMS])
                    with ExitStack() as qs_stack:
                        qs = sb(qs_stack, f"qs{n}", [NODE_TILE, tiles, 3, D], BF16)
                        project(nc, c, f"proj{n}", E, [ins[f"L0_gnn_{w}{n}"] for w in "qkv"], qs, kv)
                        attend(nc, c, f"att{n}", gnn, qs, kv, acc)
                    tmp = sb(ls, f"tmp{n}", [NODE_TILE, tiles, D])
                    attended(nc, c, f"norm{n}", acc, E, tmp, ins[f"L0_gnn_ln{n}_s"], ins[f"L0_gnn_ln{n}_b"])
            gnn_out(nc, c, ins, E, X)
        row_statistics(nc, c, "stat2", X, GIN, mean, rstd, var, c.eps5)
        gate = sb(ctx, "gate", [NODE_TILE, tiles, EXPERTS])
        with ExitStack() as gs:
            row = sb(gs, "row", [NODE_TILE, tiles, ROW])
            a_dst = sb(gs, "a_dst", [NODE_TILE, tiles, FH])
            best = sb(gs, "best", [NODE_TILE, tiles, FH])
            gacc = sb(gs, "gacc", [NODE_TILE, tiles, FE + FH])
            node_info = sb(gs, "node_info", [NODE_TILE, tiles, SPLIT, 2 * FH], BF16)
            src_sb = sb(gs, "src_sb", [LANES, gat.edge_tiles, FE + FH])
            router_rows(nc, c, ins, X, mean, rstd, row, a_dst, rows)
            with semaphores(nc, ["best_started"]) as (started,), nc.Block() as block:
                @block.vector
                def _(dve):
                    dve.tensor_copy(best[:], row[:, :, FE:FE + FH]).then_inc(started, 1)
                    dve.wait_ge(started, 1)
            neighbour_max(nc, c, gat, rows, best, src_sb)
            router_weights(nc, c, row, a_dst, best, node_info, gacc)
            neighbour_sum(nc, c, gat, src_sb, node_info, gacc)
            gates(nc, c, ins, gacc, gate)
        experts(nc, c, ins, X, mean, rstd, gate)
        with semaphores(nc, ["out_stored"]) as (stored,), nc.Block() as block:
            @block.sync
            def _(sp):
                sp.dma_start(out.rearrange(TILE_ROWS, p=NODE_TILE), X[:]).then_inc(stored, 16)
                sp.wait_ge(stored, 16)


def kernel(**inputs):
    import concourse.bacc as bacc
    from concourse.bass_utils import run_bass_kernel_spmd as run

    nc = bacc.Bacc("TRN2", target_bir_lowering=False, num_devices=1)
    arrays, ins = {}, {}
    for name, value in inputs.items():
        a = np.ascontiguousarray(value)
        arrays[f"in_{name}"] = a
        ins[name] = nc.dram_tensor(f"in_{name}", a.shape, mybir.dt.from_np(a.dtype), kind="ExternalInput").ap()
    out = nc.dram_tensor("out", inputs["x"].shape, F32, kind="ExternalOutput").ap()
    program(nc, ins, out)
    r = run(nc, [arrays], core_ids=[0])
    return r.results[0]["out"]
```
